# Optimizing a Trainium2 kernel written in Bass

```python
import numpy as np
import jax
import jax.numpy as jnp

def _softmax(x, axis=-1):
    return jax.nn.softmax(x, axis=axis)

def _gelu(x):
    return jax.nn.gelu(x, approximate=True)

def _silu(x):
    return jax.nn.silu(x)

def _sigmoid(x):
    return jax.nn.sigmoid(x)

def _layernorm(x, axis=-1, eps=1e-05):
    m = jnp.mean(x, axis=axis, keepdims=True)
    v = jnp.var(x, axis=axis, keepdims=True)
    return (x - m) / jnp.sqrt(v + eps)

def _scatter_add(tgt, idx, src, axis=0):
    return tgt.at[idx].add(src)

def _segment_sum(src, seg, n):
    return jax.ops.segment_sum(src, seg, n)
kernel_name = 'mk_adaln_d2_jaxref_r8_f7e1dc'

def setup_inputs(seed: int=0):
    np.random.seed(seed)
    _w = jnp.asarray

    def _L0_attn_setup():
        import jax, jax.numpy as jnp
        import numpy as np
        D_MODEL = 256
        D_INNER = 2 * D_MODEL
        D_STATE = 16
        D_CONV = 4
        DT_RANK = D_MODEL // 16
        BATCH, SEQLEN = (2, 128)

        def _mamba_forward(hidden_states, in_proj_w, conv_w, conv_b, x_proj_w, dt_proj_w, dt_proj_b, A_log, D, out_proj_w):
            B, L, _ = hidden_states.shape
            xz = jnp.einsum('bld,ed->ble', hidden_states, in_proj_w)
            x, z = jnp.split(xz, 2, axis=-1)
            x_pad = jnp.pad(x, ((0, 0), (D_CONV - 1, 0), (0, 0)))
            windows = jnp.stack([x_pad[:, k:k + L, :] for k in range(D_CONV)], axis=-1)
            x_conv = jnp.einsum('bldk,dk->bld', windows, conv_w) + conv_b
            x_act = jax.nn.silu(x_conv)
            x_dbl = jnp.einsum('bld,ed->ble', x_act, x_proj_w)
            dt, Bc, Cc = jnp.split(x_dbl, [DT_RANK, DT_RANK + D_STATE], axis=-1)
            dt = jax.nn.softplus(jnp.einsum('blr,dr->bld', dt, dt_proj_w) + dt_proj_b)
            A = -jnp.exp(A_log)

            def step(h, inp):
                x_t, dt_t, B_t, C_t = inp
                dA = jnp.exp(dt_t[:, :, None] * A[None])
                dBx = dt_t[:, :, None] * B_t[:, None, :] * x_t[:, :, None]
                h = h * dA + dBx
                y = jnp.einsum('bdn,bn->bd', h, C_t)
                return (h, y)
            xs = (x_act.transpose(1, 0, 2), dt.transpose(1, 0, 2), Bc.transpose(1, 0, 2), Cc.transpose(1, 0, 2))
            h0 = jnp.zeros((B, D_INNER, D_STATE), x_act.dtype)
            _, ys = jax.lax.scan(step, h0, xs)
            y = ys.transpose(1, 0, 2) + x_act * D
            y = y * jax.nn.silu(z)
            return jnp.einsum('bld,md->blm', y, out_proj_w)
        key = jax.random.key(seed)
        ks = jax.random.split(key, 10)
        s = 0.02
        inp = {'hidden_states': jax.random.normal(ks[0], (BATCH, SEQLEN, D_MODEL), jnp.float32), 'in_proj_w': jax.random.normal(ks[1], (2 * D_INNER, D_MODEL), jnp.float32) * s, 'conv_w': jax.random.normal(ks[2], (D_INNER, D_CONV), jnp.float32) * s, 'conv_b': jax.random.normal(ks[3], (D_INNER,), jnp.float32) * s, 'x_proj_w': jax.random.normal(ks[4], (DT_RANK + 2 * D_STATE, D_INNER), jnp.float32) * s, 'dt_proj_w': jax.random.normal(ks[5], (D_INNER, DT_RANK), jnp.float32) * s, 'dt_proj_b': jax.random.normal(ks[6], (D_INNER,), jnp.float32) * 0.1, 'A_log': jnp.log(jnp.tile(jnp.arange(1, D_STATE + 1, dtype=jnp.float32), (D_INNER, 1))), 'D': jnp.ones((D_INNER,), jnp.float32), 'out_proj_w': jax.random.normal(ks[7], (D_MODEL, D_INNER), jnp.float32) * s}
        return inp
    _L0_attn_in = _L0_attn_setup()

    def _L0_ffn_setup():
        import jax, jax.numpy as jnp
        import numpy as np
        B, S, H, F, E, K = (2, 128, 256, 688, 8, 2)
        key = jax.random.key(seed)
        k0, k1, k2, k3, k4 = jax.random.split(key, 5)
        x = jax.random.normal(k0, (B, S, H), dtype=jnp.float32)
        router_w = jax.random.normal(k1, (E, H), dtype=jnp.float32) * 0.02
        gate_w = jax.random.normal(k2, (E, F, H), dtype=jnp.float32) * 0.02
        up_w = jax.random.normal(k3, (E, F, H), dtype=jnp.float32) * 0.02
        down_w = jax.random.normal(k4, (E, H, F), dtype=jnp.float32) * 0.02
        return {'x': x, 'router_w': router_w, 'gate_w': gate_w, 'up_w': up_w, 'down_w': down_w}
    _L0_ffn_in = _L0_ffn_setup()
    _L0_c = _w((lambda *s: np.random.randn(*s).astype(np.float32) * 0.05)(2, 256))
    _L0_wmod = _w((lambda *s: np.random.randn(*s).astype(np.float32) * 0.05)(256, 6 * 256) * 256 ** (-0.5))

    def _L1_attn_setup():
        import jax, jax.numpy as jnp
        import numpy as np
        E = 256
        H = 3
        key = jax.random.key(seed)
        ks = jax.random.split(key, 6)
        B, N = (4, 256)
        x = jax.random.normal(ks[0], (B, N, E), dtype=jnp.float32)
        Wq = jax.random.normal(ks[1], (H, E, E), dtype=jnp.float32) * 0.02
        Wk = jax.random.normal(ks[2], (H, E, E), dtype=jnp.float32) * 0.02
        Wv = jax.random.normal(ks[3], (H, E, E), dtype=jnp.float32) * 0.02
        fc_w = jax.random.normal(ks[4], (E, E), dtype=jnp.float32) * 0.02
        fc_b = jax.random.normal(ks[5], (E,), dtype=jnp.float32) * 0.02
        return {'x': x, 'Wq': Wq, 'Wk': Wk, 'Wv': Wv, 'fc_w': fc_w, 'fc_b': fc_b}
    _L1_attn_in = _L1_attn_setup()

    def _L1_ffn_setup():
        import jax, jax.numpy as jnp
        import numpy as np
        B, S, D = (2, 256, 256)
        H, KV, HD = (16, 4, 128)
        E, F, TOPK = (8, 512, 2)
        THETA = 1000000.0
        EPS = 1e-05

        def rmsnorm(x, w):
            var = jnp.mean(jnp.square(x), axis=-1, keepdims=True)
            return x * jax.lax.rsqrt(var + EPS) * w

        def rope_cos_sin(seq_len):
            inv_freq = 1.0 / THETA ** (jnp.arange(0, HD, 2, dtype=jnp.float32) / HD)
            ang = jnp.arange(seq_len, dtype=jnp.float32)[:, None] * inv_freq[None, :]
            return (jnp.cos(ang)[None, :, None, :], jnp.sin(ang)[None, :, None, :])

        def apply_rope(x, cos, sin):
            x1, x2 = jnp.split(x, 2, axis=-1)
            return jnp.concatenate([x1 * cos - x2 * sin, x2 * cos + x1 * sin], axis=-1)

        def attention(x, wq, wk, wv, wo):
            b, s, _ = x.shape
            q = (x @ wq).reshape(b, s, H, HD)
            k = (x @ wk).reshape(b, s, KV, HD)
            v = (x @ wv).reshape(b, s, KV, HD)
            cos, sin = rope_cos_sin(s)
            q = apply_rope(q, cos, sin)
            k = apply_rope(k, cos, sin)
            rep = H // KV
            k = jnp.repeat(k, rep, axis=2)
            v = jnp.repeat(v, rep, axis=2)
            scores = jnp.einsum('bqhd,bkhd->bhqk', q, k) / np.sqrt(HD)
            causal = jnp.tril(jnp.ones((s, s), dtype=bool))
            scores = jnp.where(causal[None, None], scores, jnp.finfo(scores.dtype).min)
            probs = jax.nn.softmax(scores, axis=-1)
            out = jnp.einsum('bhqk,bkhd->bqhd', probs, v).reshape(b, s, H * HD)
            return out @ wo

        def moe(x, gate_w, w1, w3, w2):
            b, s, d = x.shape
            xt = x.reshape(b * s, d)
            logits = xt @ gate_w
            topv, topi = jax.lax.top_k(logits, TOPK)
            probs = jax.nn.softmax(topv, axis=-1)
            w = jnp.zeros_like(logits)
            for kk in range(TOPK):
                w = w + jax.nn.one_hot(topi[:, kk], E, dtype=logits.dtype) * probs[:, kk:kk + 1]
            out = jnp.zeros_like(xt)
            for e in range(E):
                h = jax.nn.silu(xt @ w1[e]) * (xt @ w3[e])
                out = out + w[:, e:e + 1] * (h @ w2[e])
            return out.reshape(b, s, d)
        key = jax.random.key(seed)
        ks = jax.random.split(key, 10)
        init = lambda k, shape: jax.random.normal(k, shape, jnp.float32) * 0.02
        return {'hidden_states': jax.random.normal(ks[0], (B, S, D), jnp.float32), 'norm1_w': jnp.ones((D,), jnp.float32), 'norm2_w': jnp.ones((D,), jnp.float32), 'wq': init(ks[1], (D, H * HD)), 'wk': init(ks[2], (D, KV * HD)), 'wv': init(ks[3], (D, KV * HD)), 'wo': init(ks[4], (H * HD, D)), 'gate_w': init(ks[5], (D, E)), 'w1': init(ks[6], (E, D, F)), 'w3': init(ks[7], (E, D, F)), 'w2': init(ks[8], (E, F, D))}
    _L1_ffn_in = _L1_ffn_setup()
    _L1_c = _w((lambda *s: np.random.randn(*s).astype(np.float32) * 0.05)(2, 256))
    _L1_wmod = _w((lambda *s: np.random.randn(*s).astype(np.float32) * 0.05)(256, 6 * 256) * 256 ** (-0.5))
    _d = {'L0_attn_hidden_states': _L0_attn_in['hidden_states'], 'L0_attn_in_proj_w': _L0_attn_in['in_proj_w'], 'L0_attn_conv_w': _L0_attn_in['conv_w'], 'L0_attn_conv_b': _L0_attn_in['conv_b'], 'L0_attn_x_proj_w': _L0_attn_in['x_proj_w'], 'L0_attn_dt_proj_w': _L0_attn_in['dt_proj_w'], 'L0_attn_dt_proj_b': _L0_attn_in['dt_proj_b'], 'L0_attn_A_log': _L0_attn_in['A_log'], 'L0_attn_D': _L0_attn_in['D'], 'L0_attn_out_proj_w': _L0_attn_in['out_proj_w'], 'L0_ffn_router_w': _L0_ffn_in['router_w'], 'L0_ffn_gate_w': _L0_ffn_in['gate_w'], 'L0_ffn_up_w': _L0_ffn_in['up_w'], 'L0_ffn_down_w': _L0_ffn_in['down_w'], 'L0_c': _L0_c, 'L0_wmod': _L0_wmod, 'L1_attn_Wq': _L1_attn_in['Wq'], 'L1_attn_Wk': _L1_attn_in['Wk'], 'L1_attn_Wv': _L1_attn_in['Wv'], 'L1_attn_fc_w': _L1_attn_in['fc_w'], 'L1_attn_fc_b': _L1_attn_in['fc_b'], 'L1_ffn_norm1_w': _L1_ffn_in['norm1_w'], 'L1_ffn_norm2_w': _L1_ffn_in['norm2_w'], 'L1_ffn_wq': _L1_ffn_in['wq'], 'L1_ffn_wk': _L1_ffn_in['wk'], 'L1_ffn_wv': _L1_ffn_in['wv'], 'L1_ffn_wo': _L1_ffn_in['wo'], 'L1_ffn_gate_w': _L1_ffn_in['gate_w'], 'L1_ffn_w1': _L1_ffn_in['w1'], 'L1_ffn_w3': _L1_ffn_in['w3'], 'L1_ffn_w2': _L1_ffn_in['w2'], 'L1_c': _L1_c, 'L1_wmod': _L1_wmod}
    _x0 = _d['L0_attn_hidden_states']
    _d['L0_attn_hidden_states'] = jax.random.normal(jax.random.fold_in(jax.random.key(seed), 1), (2, 1024, 256), dtype=_x0.dtype)
    del _x0
    return _d

def reference(L0_attn_hidden_states, L0_attn_in_proj_w, L0_attn_conv_w, L0_attn_conv_b, L0_attn_x_proj_w, L0_attn_dt_proj_w, L0_attn_dt_proj_b, L0_attn_A_log, L0_attn_D, L0_attn_out_proj_w, L0_ffn_router_w, L0_ffn_gate_w, L0_ffn_up_w, L0_ffn_down_w, L0_c, L0_wmod, L1_attn_Wq, L1_attn_Wk, L1_attn_Wv, L1_attn_fc_w, L1_attn_fc_b, L1_ffn_norm1_w, L1_ffn_norm2_w, L1_ffn_wq, L1_ffn_wk, L1_ffn_wv, L1_ffn_wo, L1_ffn_gate_w, L1_ffn_w1, L1_ffn_w3, L1_ffn_w2, L1_c, L1_wmod):

    def _L0_attn_ref(hidden_states, in_proj_w, conv_w, conv_b, x_proj_w, dt_proj_w, dt_proj_b, A_log, D, out_proj_w):
        import jax, jax.numpy as jnp
        import numpy as np
        D_MODEL = 256
        D_INNER = 2 * D_MODEL
        D_STATE = 16
        D_CONV = 4
        DT_RANK = D_MODEL // 16
        BATCH, SEQLEN = (2, 128)

        def _mamba_forward(hidden_states, in_proj_w, conv_w, conv_b, x_proj_w, dt_proj_w, dt_proj_b, A_log, D, out_proj_w):
            B, L, _ = hidden_states.shape
            xz = jnp.einsum('bld,ed->ble', hidden_states, in_proj_w)
            x, z = jnp.split(xz, 2, axis=-1)
            x_pad = jnp.pad(x, ((0, 0), (D_CONV - 1, 0), (0, 0)))
            windows = jnp.stack([x_pad[:, k:k + L, :] for k in range(D_CONV)], axis=-1)
            x_conv = jnp.einsum('bldk,dk->bld', windows, conv_w) + conv_b
            x_act = jax.nn.silu(x_conv)
            x_dbl = jnp.einsum('bld,ed->ble', x_act, x_proj_w)
            dt, Bc, Cc = jnp.split(x_dbl, [DT_RANK, DT_RANK + D_STATE], axis=-1)
            dt = jax.nn.softplus(jnp.einsum('blr,dr->bld', dt, dt_proj_w) + dt_proj_b)
            A = -jnp.exp(A_log)

            def step(h, inp):
                x_t, dt_t, B_t, C_t = inp
                dA = jnp.exp(dt_t[:, :, None] * A[None])
                dBx = dt_t[:, :, None] * B_t[:, None, :] * x_t[:, :, None]
                h = h * dA + dBx
                y = jnp.einsum('bdn,bn->bd', h, C_t)
                return (h, y)
            xs = (x_act.transpose(1, 0, 2), dt.transpose(1, 0, 2), Bc.transpose(1, 0, 2), Cc.transpose(1, 0, 2))
            h0 = jnp.zeros((B, D_INNER, D_STATE), x_act.dtype)
            _, ys = jax.lax.scan(step, h0, xs)
            y = ys.transpose(1, 0, 2) + x_act * D
            y = y * jax.nn.silu(z)
            return jnp.einsum('bld,md->blm', y, out_proj_w)
        return _mamba_forward(hidden_states, in_proj_w, conv_w, conv_b, x_proj_w, dt_proj_w, dt_proj_b, A_log, D, out_proj_w)

    def _L0_ffn_ref(x, router_w, gate_w, up_w, down_w):
        import jax, jax.numpy as jnp
        import numpy as np
        B, S, H, F, E, K = (2, 128, 256, 688, 8, 2)
        b, s, h = x.shape
        xf = x.reshape(-1, h)
        logits = xf @ router_w.T
        top_v, top_i = jax.lax.top_k(logits, K)
        probs = jax.nn.softmax(top_v.astype(jnp.float32), axis=-1).astype(logits.dtype)
        combine = jnp.sum(jax.nn.one_hot(top_i, E, dtype=x.dtype) * probs[..., None], axis=1)
        g = jnp.einsum('th,efh->etf', xf, gate_w)
        u = jnp.einsum('th,efh->etf', xf, up_w)
        y = jnp.einsum('etf,ehf->eth', jax.nn.silu(g) * u, down_w)
        out = jnp.einsum('te,eth->th', combine, y)
        return out.reshape(b, s, h)

    def _L1_attn_ref(x, Wq, Wk, Wv, fc_w, fc_b):
        import jax, jax.numpy as jnp
        import numpy as np
        E = 256
        H = 3
        Q = jnp.einsum('bne,hde->hbnd', x, Wq)
        K = jnp.einsum('bne,hde->hbnd', x, Wk)
        V = jnp.einsum('bne,hde->hbnd', x, Wv)
        scale = 1.0 / jnp.sqrt(jnp.float32(E))
        scores = jnp.einsum('hbnd,hbmd->hbnm', Q, K) * scale
        w = jax.nn.softmax(scores, axis=2)
        attn = jnp.einsum('hbnm,hbmd->hbnd', w, V)
        mean = jnp.mean(attn, axis=0)
        return mean @ fc_w.T + fc_b

    def _L1_ffn_ref(hidden_states, norm1_w, norm2_w, wq, wk, wv, wo, gate_w, w1, w3, w2):
        import jax, jax.numpy as jnp
        import numpy as np
        B, S, D = (2, 256, 256)
        H, KV, HD = (16, 4, 128)
        E, F, TOPK = (8, 512, 2)
        THETA = 1000000.0
        EPS = 1e-05

        def rmsnorm(x, w):
            var = jnp.mean(jnp.square(x), axis=-1, keepdims=True)
            return x * jax.lax.rsqrt(var + EPS) * w

        def rope_cos_sin(seq_len):
            inv_freq = 1.0 / THETA ** (jnp.arange(0, HD, 2, dtype=jnp.float32) / HD)
            ang = jnp.arange(seq_len, dtype=jnp.float32)[:, None] * inv_freq[None, :]
            return (jnp.cos(ang)[None, :, None, :], jnp.sin(ang)[None, :, None, :])

        def apply_rope(x, cos, sin):
            x1, x2 = jnp.split(x, 2, axis=-1)
            return jnp.concatenate([x1 * cos - x2 * sin, x2 * cos + x1 * sin], axis=-1)

        def attention(x, wq, wk, wv, wo):
            b, s, _ = x.shape
            q = (x @ wq).reshape(b, s, H, HD)
            k = (x @ wk).reshape(b, s, KV, HD)
            v = (x @ wv).reshape(b, s, KV, HD)
            cos, sin = rope_cos_sin(s)
            q = apply_rope(q, cos, sin)
            k = apply_rope(k, cos, sin)
            rep = H // KV
            k = jnp.repeat(k, rep, axis=2)
            v = jnp.repeat(v, rep, axis=2)
            scores = jnp.einsum('bqhd,bkhd->bhqk', q, k) / np.sqrt(HD)
            causal = jnp.tril(jnp.ones((s, s), dtype=bool))
            scores = jnp.where(causal[None, None], scores, jnp.finfo(scores.dtype).min)
            probs = jax.nn.softmax(scores, axis=-1)
            out = jnp.einsum('bhqk,bkhd->bqhd', probs, v).reshape(b, s, H * HD)
            return out @ wo

        def moe(x, gate_w, w1, w3, w2):
            b, s, d = x.shape
            xt = x.reshape(b * s, d)
            logits = xt @ gate_w
            topv, topi = jax.lax.top_k(logits, TOPK)
            probs = jax.nn.softmax(topv, axis=-1)
            w = jnp.zeros_like(logits)
            for kk in range(TOPK):
                w = w + jax.nn.one_hot(topi[:, kk], E, dtype=logits.dtype) * probs[:, kk:kk + 1]
            out = jnp.zeros_like(xt)
            for e in range(E):
                h = jax.nn.silu(xt @ w1[e]) * (xt @ w3[e])
                out = out + w[:, e:e + 1] * (h @ w2[e])
            return out.reshape(b, s, d)
        attn_out = attention(rmsnorm(hidden_states, norm1_w), wq, wk, wv, wo)
        h = hidden_states + attn_out
        out = h + moe(rmsnorm(h, norm2_w), gate_w, w1, w3, w2)
        return out
    x = L0_attn_hidden_states
    mod = (_silu(L0_c) @ L0_wmod).reshape(L0_c.shape[0], 6, 1, -1)
    sa, ca, ga, sb, cb, gb = (mod[:, 0], mod[:, 1], mod[:, 2], mod[:, 3], mod[:, 4], mod[:, 5])
    ga = (2 * (ga >= 0) - 1) * jnp.maximum(jnp.abs(ga), 0.25)
    gb = (2 * (gb >= 0) - 1) * jnp.maximum(jnp.abs(gb), 0.25)
    h = _layernorm(x, axis=-1) * (1 + ca) + sa
    x = x + ga * _L0_attn_ref(h, L0_attn_in_proj_w, L0_attn_conv_w, L0_attn_conv_b, L0_attn_x_proj_w, L0_attn_dt_proj_w, L0_attn_dt_proj_b, L0_attn_A_log, L0_attn_D, L0_attn_out_proj_w)
    h = _layernorm(x, axis=-1) * (1 + cb) + sb
    x = x + gb * _L0_ffn_ref(h, L0_ffn_router_w, L0_ffn_gate_w, L0_ffn_up_w, L0_ffn_down_w)
    mod = (_silu(L1_c) @ L1_wmod).reshape(L1_c.shape[0], 6, 1, -1)
    sa, ca, ga, sb, cb, gb = (mod[:, 0], mod[:, 1], mod[:, 2], mod[:, 3], mod[:, 4], mod[:, 5])
    ga = (2 * (ga >= 0) - 1) * jnp.maximum(jnp.abs(ga), 0.25)
    gb = (2 * (gb >= 0) - 1) * jnp.maximum(jnp.abs(gb), 0.25)
    h = _layernorm(x, axis=-1) * (1 + ca) + sa
    x = x + ga * _L1_attn_ref(h, L1_attn_Wq, L1_attn_Wk, L1_attn_Wv, L1_attn_fc_w, L1_attn_fc_b)
    h = _layernorm(x, axis=-1) * (1 + cb) + sb
    x = x + gb * _L1_ffn_ref(h, L1_ffn_norm1_w, L1_ffn_norm2_w, L1_ffn_wq, L1_ffn_wk, L1_ffn_wv, L1_ffn_wo, L1_ffn_gate_w, L1_ffn_w1, L1_ffn_w3, L1_ffn_w2)
    return x

_drawn_inputs = setup_inputs


def setup_inputs(seed=0):
    import zlib

    import numpy as np

    out = dict(_drawn_inputs(seed))
    spreads = {'L0_attn_D': (1.0, 0.6), 'L1_ffn_norm1_w': (1.0, 0.6), 'L1_ffn_norm2_w': (1.0, 0.6)}
    factors = {'L0_attn_in_proj_w': 8.0,
     'L0_attn_conv_w': 8.0,
     'L0_attn_conv_b': 8.0,
     'L0_attn_x_proj_w': 8.0,
     'L0_attn_dt_proj_w': 8.0,
     'L0_attn_dt_proj_b': 8.0,
     'L0_attn_A_log': 8.0,
     'L0_attn_out_proj_w': 8.0,
     'L0_ffn_router_w': 8.0,
     'L0_ffn_gate_w': 8.0,
     'L0_ffn_up_w': 8.0,
     'L0_ffn_down_w': 8.0,
     'L0_c': 8.0,
     'L0_wmod': 8.0,
     'L1_attn_Wq': 8.0,
     'L1_attn_Wk': 8.0,
     'L1_attn_Wv': 8.0,
     'L1_attn_fc_w': 8.0,
     'L1_attn_fc_b': 27.96,
     'L1_ffn_wq': 8.0,
     'L1_ffn_wk': 8.0,
     'L1_ffn_wv': 8.0,
     'L1_ffn_wo': 8.0,
     'L1_ffn_gate_w': 8.0,
     'L1_ffn_w1': 8.0,
     'L1_ffn_w3': 8.0,
     'L1_ffn_w2': 8.0}
    for name, (base, spread) in spreads.items():
        noise = np.random.default_rng([zlib.crc32(name.encode()), seed]).standard_normal(out[name].shape)
        drawn = base * np.exp(spread * noise) if base else spread * noise
        out[name] = jnp.asarray(drawn.astype(out[name].dtype))
    for name, factor in factors.items():
        out[name] = (out[name] * factor).astype(out[name].dtype)
    return out
```

```python
from contextlib import ExitStack, contextmanager

import numpy as np

import concourse.bass as bass
from concourse import mybir

P = 128
F32 = mybir.dt.float32
BF16 = mybir.dt.bfloat16
I32 = mybir.dt.int32
U32 = mybir.dt.uint32
ALU = mybir.AluOpType
ACT = mybir.ActivationFunctionType
AX_X = mybir.AxisListType.X

B, L, D = 2, 1024, 256
NT = B * L // P
TB = L // P
KC = D // P
EPS = 1e-5
DI, NS, DTR, DC = 512, 16, 16, 4
CD = DI // P
EXP = 8
SLOT_TILES = 40
AH = 3
H, KV, HD = 16, 4, 128
REP = H // KV
SA, CA, GA, SB, CB, GB = range(6)


class Own:

    def __init__(self, eng, sem):
        self.eng, self.sem, self.base, self.n = eng, sem, 0, 0

    def mark(self, ins):
        ins.then_inc(self.sem, 1)
        self.n += 1

    def wait(self):
        self.eng.wait_ge(self.sem, self.base + self.n)

    def __call__(self, ins):
        self.mark(ins)
        self.wait()

    @contextmanager
    def turn(self, i, count, per):
        base, n = self.base, self.n
        self.base, self.n = base + n + i * per, 0
        yield
        assert self.n == per, self.n
        self.base, self.n = base, n + count * per


def ds(i, n=1):
    return bass.ds(i, n)


def after(eng, sem, n):
    if not isinstance(n, int) or n > 0:
        eng.wait_ge(sem, n)


def flat(ap):
    return ap.rearrange("p a b -> p (a b)")



def dve_rstd(dve, own, src, nrm, s_var, s_sd, turn, rms):
    st, mean, var, sd, rstd, t = nrm
    for j in range(NT):
        own.mark(dve.bn_stats(st[:, j, :], src[:, j, :]))
    own.wait()
    own(dve.tensor_tensor(mean[:, :], st[:, :, 1], st[:, :, 4], ALU.add))
    own(dve.tensor_tensor(t[:, :], st[:, :, 1], st[:, :, 4], ALU.subtract))
    own(dve.scalar_tensor_tensor(t[:, :], t[:, :], 0.25, t[:, :], ALU.mult, ALU.mult))
    own(dve.tensor_tensor(var[:, :], st[:, :, 2], st[:, :, 5], ALU.add))
    own(dve.scalar_tensor_tensor(var[:, :], var[:, :], 1.0 / D, t[:, :], ALU.mult, ALU.add))
    own(dve.tensor_scalar(mean[:, :], mean[:, :], 0.5, None, ALU.mult))
    if rms:
        own(dve.tensor_tensor(t[:, :], mean[:, :], mean[:, :], ALU.mult))
        own(dve.tensor_tensor(var[:, :], var[:, :], t[:, :], ALU.add))
    dve.tensor_scalar(var[:, :], var[:, :], EPS, None, ALU.add).then_inc(s_var, 1)
    dve.wait_ge(s_sd, turn)
    own(dve.reciprocal(rstd[:, :], sd[:, :]))
    own(dve.tensor_tensor(t[:, :], var[:, :], rstd[:, :], ALU.mult))
    own(dve.tensor_tensor(t[:, :], t[:, :], rstd[:, :], ALU.mult))
    own(dve.tensor_scalar(t[:, :], t[:, :], -0.5, 1.5, ALU.mult, ALU.add))
    own(dve.tensor_tensor(rstd[:, :], rstd[:, :], t[:, :], ALU.mult))


def act_sqrt(act, nrm, s_var, s_sd, turn):
    st, mean, var, sd, rstd, t = nrm
    act.wait_ge(s_var, turn)
    act.activation(sd[:, :], var[:, :], ACT.Sqrt).then_inc(s_sd, 1)


def norm_buffers(sb, tag):
    return (sb(f"{tag}_st", [P, NT, 6]), sb(f"{tag}_mean", [P, NT]), sb(f"{tag}_var", [P, NT]),
            sb(f"{tag}_sd", [P, NT]), sb(f"{tag}_rstd", [P, NT]), sb(f"{tag}_t", [P, NT]))


def over(ap, n):
    p, d = ap.shape
    return ap.rearrange("p (a d) -> p a d", a=1).to_broadcast([p, n, d])


def modvec(mod, b, which):
    return mod[:, ds(b), ds(which * D, D)].rearrange("p a d -> p (a d)")



def modulation(nc, g, layer, c_in, wmod, first=None):
    ctx = ExitStack()
    with ctx:
        sb = lambda n, s, d=F32: ctx.enter_context(nc.sbuf_tensor(f"m{layer}_{n}", s, d))
        sem = lambda n: ctx.enter_context(nc.semaphore(f"m{layer}_{n}"))
        cT, sc, w = sb("cT", [P, KC, B]), sb("sc", [P, KC, B]), sb("w", [P, KC, 6 * D])
        sign, size = sb("sign", [P, B, 2, D]), sb("size", [P, B, 2, D])
        s_in, s_silu, s_mm, s_raw, s_own, s_x = (sem(n) for n in ("in", "silu", "mm", "raw", "own", "x"))
        mod, ps = g.mod, g.ps
        block = ctx.enter_context(nc.Block())

        @block.sync
        def _(sp):
            with nc.allow_non_contiguous_dma(reason="256 values"):
                for b in range(B):
                    for k in range(KC):
                        sp.dma_start(cT[:, k, b:b + 1], c_in[b, k * P:(k + 1) * P].rearrange("(p a) -> p a", a=1)).then_inc(s_in, 16)
            sp.dma_start(w[:, :, :], wmod.rearrange("(k p) n -> p k n", p=P)).then_inc(s_in, 16)
            if first is not None:
                n = first(sp, s_x)
                sp.wait_ge(s_x, 16 * n)

        @block.scalar
        def _(act):
            act.wait_ge(s_in, 16 * (B * KC + 1))
            act.activation(sc[:, :, :], cT[:, :, :], ACT.Silu).then_inc(s_silu, 1)
            for b in range(B):
                act.wait_ge(s_mm, b + 1)
                act.activation(mod[:, b, :], ps[:, 4 * b:4 * b + 3, :].rearrange("p a n -> p (a n)"),
                               ACT.Copy).then_inc(s_raw, 1)

        @block.tensor
        def _(pe):
            pe.wait_ge(s_silu, 1)
            for b in range(B):
                for n in range(3):
                    for k in range(KC):
                        mm = pe.matmul(ps[:, 4 * b + n, :], sc[:, k, b:b + 1].to_broadcast([P, P]),
                                       w[:, k, n * 512:(n + 1) * 512], start=(k == 0), stop=(k == KC - 1))
                mm.then_inc(s_mm, 1)

        @block.vector
        def _(dve):
            own = Own(dve, s_own)
            dve.wait_ge(s_raw, B)
            v = mod[:, :, :].rearrange("p b (s d) -> p b s d", s=6)
            own.mark(dve.tensor_scalar(v[:, :, 1:6:3, :], v[:, :, 1:6:3, :], 1.0, None, ALU.add))
            own.mark(dve.tensor_scalar(sign[:, :, :, :], v[:, :, 2:6:3, :], 0.0, 2.0, ALU.is_ge, ALU.mult))
            for b in range(B):
                own(dve.scalar_tensor_tensor(size[:, b, :, :], v[:, b, 2:6:3, :], -1.0, v[:, b, 2:6:3, :],
                                             ALU.mult, ALU.max))
            own(dve.tensor_scalar(size[:, :, :, :], size[:, :, :, :], 0.25, None, ALU.max))
            for b in range(B):
                own(dve.scalar_tensor_tensor(v[:, b, 2:6:3, :], sign[:, b, :, :], 1.0, size[:, b, :, :],
                                             ALU.subtract, ALU.mult))



def mamba(nc, g, w_in, conv_w, conv_b, xproj, dtw, dtb, a_log, dskip, w_out):
    ctx = ExitStack()
    with ctx:
        sb = lambda n, s, d=F32: ctx.enter_context(nc.sbuf_tensor(f"mb_{n}", s, d))
        sem = lambda n: ctx.enter_context(nc.semaphore(f"mb_{n}"))
        x, mod, ps, ident = g.x, g.mod, g.ps, g.ident
        win = sb("win", [P, KC, 2 * DI])
        wx = sb("wx", [P, CD, 2 * NS + DTR])
        wdt = sb("wdt", [DTR, DI])
        wout = sb("wout", [P, CD, D])
        cw, cb, db, dsk = sb("cw", [P, CD, DC]), sb("cb", [P, CD]), sb("db", [P, CD]), sb("dsk", [P, CD])
        am = sb("am", [P, CD, NS])
        sel, sel_f = sb("sel", [96, 32], BF16), sb("sel_f", [96, 32])
        nrm = norm_buffers(sb, "mb_n")
        xp = sb("xp", [P, CD, L + DC - 1])
        z, xa, u = sb("z", [P, CD, L]), sb("xa", [P, CD, L]), sb("u", [P, CD, L])
        bb = sb("bb", [P, NS, L])
        xn = bb[:, 0:2, :].rearrange("p a (t d) -> p (a t) d", d=D)
        hT = bb[:, 2:4, :]
        xc = bb[:, 4:8, :]
        relu_v = bb[:, 4:8, :]
        abs_v = bb[:, 8:12, :]
        rest = bb[0:32, 15, :]
        xdt = sb("xdt", [DTR, L])
        mid = sb("mid", [32, L], BF16)
        parts = sb("parts", [96, L], BF16)
        dbx, h = sb("dbx", [P, 2, L]), sb("h", [P, 2, L])

        s_in = sem("in")
        s_own = sem("own")
        s_sel = sem("sel")
        s_pad = sem("pad")
        s_am, s_var, s_sd = sem("am"), sem("var"), sem("sd")
        s_xn = sem("xn")
        s_tr, s_hT = sem("tr"), sem("hT")
        s_ip = sem("ip")
        s_xp, s_z = sem("xp"), sem("z")
        s_tap, s_conv, s_xa = sem("tap"), sem("conv"), sem("xa")
        s_xd, s_parts = sem("xd"), sem("parts")
        s_dt = sem("dt")
        s_abs, s_exp, s_log, s_u = sem("abs"), sem("exp"), sem("log"), sem("u")
        s_bps, s_bb = sem("bps"), sem("bb")
        s_c, s_da, s_dbx = sem("c"), sem("da"), sem("dbx")
        s_g, s_y, s_gated = sem("g"), sem("y"), sem("gated")
        s_op, s_res = sem("op"), sem("res")
        block = ctx.enter_context(nc.Block())

        def pair(i):
            return flat(ps[:, 2 * i:2 * i + 2, :])

        @block.sync
        def _(sp):
            loads = [(win[:, :, :], w_in.rearrange("(k p) n -> p k n", p=P)),
                     (wx[:, :, :], xproj.rearrange("(k p) n -> p k n", p=P)),
                     (wdt[:, :], dtw), (wout[:, :, :], w_out.rearrange("(k p) n -> p k n", p=P)),
                     (cw[:, :, :], conv_w.rearrange("(k p) n -> p k n", p=P)),
                     (cb[:, :], conv_b), (db[:, :], dtb), (dsk[:, :], dskip),
                     (am[:, :, :], a_log.rearrange("(k p) n -> p k n", p=P)), (sel_f[:, :], g.sel_dram)]
            for dst, src in loads:
                sp.dma_start(dst, src).then_inc(s_in, 16)
            sp.wait_ge(s_in, 16 * len(loads))

        LOADED = 160

        @block.vector
        def _(dve):
            own = Own(dve, s_own)
            for primed in (s_g, s_gated, s_res):
                dve.sem_inc(primed, 1)
            dve.memset(xp[:, :, 0:DC - 1], 0.0).then_inc(s_pad, 1)
            dve_rstd(dve, own, x, nrm, s_var, s_sd, 1, False)
            dve.wait_ge(s_in, LOADED)
            dve.tensor_copy(sel[:, :], sel_f[:, :]).then_inc(s_sel, 1)
            dve.wait_ge(s_am, 1)
            own(dve.tensor_scalar(am[:, :, :], am[:, :, :], -1.0, None, ALU.mult))
            with dve.Fori(0, B) as b, own.turn(b, B, TB + 1 + CD * 2 + 4 + CD + CD * (NS + 1) + TB):
                st, mean, var, sd, rstd, t = nrm
                for j in range(TB):
                    c = b * TB + j
                    own.mark(dve.tensor_scalar(xn[:, j, :], flat(x[:, ds(c), :]), mean[:, ds(c)], rstd[:, ds(c)],
                                               ALU.subtract, ALU.mult))
                own.wait()
                own(dve.tensor_tensor(xn, xn, over(modvec(mod, b, CA), TB), ALU.mult))
                dve.tensor_tensor(xn, xn, over(modvec(mod, b, SA), TB), ALU.add).then_inc(s_xn, 1)
                for k in range(CD):
                    dve.wait_ge(s_tap, b * CD + k + 1)
                    for tap in range(DC - 1):
                        ins = dve.scalar_tensor_tensor(xc[:, k, :], xp[:, k, tap:tap + L], cw[:, k, tap:tap + 1],
                                                       xc[:, k, :], ALU.mult, ALU.add)
                        if tap < DC - 2:
                            own(ins)
                        else:
                            ins.then_inc(s_conv, 1)
                dve.wait_ge(s_xd, b + 1)
                bc = flat(ps[0:32, 0:2, :])
                own.mark(dve.tensor_copy(xdt[:, :], flat(ps[32:48, 0:2, :])))
                own(dve.tensor_copy(parts[0:32, :], bc))
                own(dve.tensor_tensor(rest, bc, parts[0:32, :], ALU.subtract))
                own(dve.tensor_copy(mid[:, :], rest))
                dve.tensor_copy(parts[32:64, :], mid[:, :])
                dve.tensor_tensor(parts[64:96, :], rest, mid[:, :], ALU.subtract).then_inc(s_parts, 1)
                for k in range(CD):
                    dve.wait_ge(s_log, b * CD + k + 1)
                    own(dve.tensor_tensor(xp[:, k, DC - 1:], relu_v[:, k, :], abs_v[:, k, :], ALU.add))
                    dve.tensor_tensor(u[:, k, :], xp[:, k, DC - 1:], xa[:, k, :], ALU.mult).then_inc(s_u, 1)
                with dve.Fori(0, CD) as k, own.turn(k, CD, NS + 1):
                    for n in range(NS):
                        at = (b * CD + k) * NS + n
                        dve.wait_ge(s_da, at + 1)
                        dve.wait_ge(s_dbx, at + 1)
                        if n >= 2:
                            dve.wait_ge(s_y, at - 1)
                        own.mark(dve.tensor_tensor_scan(h[:, n % 2, :], pair(2 + n % 2), dbx[:, n % 2, :], 0.0,
                                                        ALU.mult, ALU.add))
                        dve.wait_ge(s_c, at + 1)
                        own.wait()
                        dve.tensor_tensor(h[:, n % 2, :], h[:, n % 2, :], pair(0), ALU.mult).then_inc(s_g, 1)
                    dve.wait_ge(s_y, (b * CD + k) * NS + NS)
                    dve.wait_ge(s_z, b * 8 + 8)
                    xk = flat(xa[:, ds(k), :])
                    own(dve.scalar_tensor_tensor(xk, xk, dsk[:, ds(k)], pair(1), ALU.mult, ALU.add))
                    dve.tensor_tensor(xk, xk, flat(z[:, ds(k), :]), ALU.mult).then_inc(s_gated, 1)
                for j in range(TB):
                    dve.wait_ge(s_op, b * TB + j + 1)
                    if j:
                        dve.wait_ge(s_res, 1 + b * TB + j)
                    xj = flat(x[:, ds(b * TB + j), :])
                    own(dve.tensor_tensor(h[:, 0, 0:D], ps[:, j, 0:D], modvec(mod, b, GA), ALU.mult))
                    dve.tensor_tensor(xj, xj, h[:, 0, 0:D], ALU.add).then_inc(s_res, 1)
                dve.wait_ge(s_res, 1 + b * TB + TB)

        @block.scalar
        def _(act):
            act_sqrt(act, nrm, s_var, s_sd, 1)
            act.wait_ge(s_in, LOADED)
            act.activation(am[:, :, :], am[:, :, :], ACT.Exp).then_inc(s_am, 1)
            act.wait_ge(s_pad, 1)
            with act.Fori(0, B) as b:
                for q in range(4):
                    act.wait_ge(s_tr, b * 4 + q + 1)
                    act.activation(hT[:, q // 2, (q % 2) * 512:(q % 2) * 512 + 512], ps[:, q, :], ACT.Copy).then_inc(s_hT, 1)
                for e in range(16):
                    act.wait_ge(s_ip, b * 16 + e + 1)
                    c, t = e // 2, e % 2
                    if c < CD:
                        act.activation(xp[:, c, DC - 1 + t * 512:DC - 1 + (t + 1) * 512], ps[:, e % 8, :],
                                       ACT.Copy).then_inc(s_xp, 1)
                    else:
                        act.activation(z[:, c - CD, t * 512:(t + 1) * 512], ps[:, e % 8, :], ACT.Silu).then_inc(s_z, 1)
                    if c < CD and t:
                        act.wait_ge(s_xp, b * 8 + e + 1)
                        act.activation(xc[:, c, :], xp[:, c, DC - 1:], ACT.Identity, bias=cb[:, c:c + 1],
                                       scale=cw[:, c, DC - 1:DC]).then_inc(s_tap, 1)
                for k in range(CD):
                    act.wait_ge(s_conv, b * CD + k + 1)
                    act.activation(xa[:, k, :], xc[:, k, :], ACT.Silu).then_inc(s_xa, 1)
                for k in range(CD):
                    act.wait_ge(s_dt, b * CD + k + 1)
                    act.activation(relu_v[:, k, :], pair(1 + k % 2), ACT.Relu, bias=db[:, k:k + 1])
                    act.activation(abs_v[:, k, :], pair(1 + k % 2), ACT.Abs, bias=db[:, k:k + 1]).then_inc(s_abs, 1)
                for k in range(CD):
                    act.wait_ge(s_abs, b * CD + k + 1)
                    act.activation(abs_v[:, k, :], abs_v[:, k, :], ACT.Exp, scale=-1.0).then_inc(s_exp, 1)
                for k in range(CD):
                    act.wait_ge(s_exp, b * CD + k + 1)
                    act.activation(abs_v[:, k, :], abs_v[:, k, :], ACT.Ln, bias=1.0).then_inc(s_log, 1)
                act.wait_ge(s_u, b * CD + CD)
                for n in range(NS):
                    act.wait_ge(s_bps, b * NS + n + 1)
                    act.activation(bb[:, n, :], pair(n % 4), ACT.Copy).then_inc(s_bb, 1)
                act.wait_ge(s_bb, b * NS + NS)
                with act.Fori(0, CD) as k:
                    act.wait_ge(s_gated, 1 + b * CD + k)
                    for n in range(NS):
                        at = (b * CD + k) * NS + n
                        if n >= 2:
                            act.wait_ge(s_g, 1 + at - 1)
                        act.activation(pair(2 + n % 2), flat(xp[:, ds(k), DC - 1:]), ACT.Exp,
                                       scale=flat(am[:, ds(k), n:n + 1])).then_inc(s_da, 1)

        @block.gpsimd
        def _(pool):
            with pool.Fori(0, B) as b:
                for k in range(CD):
                    pool.wait_ge(s_gated, 1 + b * CD + k)
                    for n in range(NS):
                        at = (b * CD + k) * NS + n
                        pool.wait_ge(s_bb, b * NS + n + 1)
                        if n >= 2:
                            pool.wait_ge(s_g, 1 + at - 1)
                        pool.tensor_tensor(dbx[:, n % 2, :], u[:, k, :], bb[:, n, :], ALU.mult).then_inc(s_dbx, 1)

        @block.tensor
        def _(pe):
            pe.wait_ge(s_in, LOADED)
            pe.wait_ge(s_sel, 1)
            with pe.Fori(0, B) as b:
                pe.wait_ge(s_xn, b + 1)
                pe.wait_ge(s_res, 1 + b * TB)
                for q in range(4):
                    for j in range(4):
                        tr = pe.transpose(ps[:, q, j * P:(j + 1) * P],
                                          xn[:, 4 * (q % 2) + j, (q // 2) * P:(q // 2 + 1) * P], ident[:, :])
                    tr.then_inc(s_tr, 1)
                pe.wait_ge(s_hT, b * 4 + 4)
                for e in range(16):
                    if e >= 8:
                        pe.wait_ge(s_xp, b * 8 + e - 7)
                    c, t = e // 2, e % 2
                    for k in range(KC):
                        mm = pe.matmul(ps[:, e % 8, :], win[:, k, c * P:(c + 1) * P], hT[:, k, t * 512:(t + 1) * 512],
                                       start=(k == 0), stop=(k == KC - 1))
                    mm.then_inc(s_ip, 1)
                pe.wait_ge(s_z, b * 8 + 8)
                for k in range(CD):
                    pe.wait_ge(s_xa, b * CD + k + 1)
                    for t in range(2):
                        mm = pe.matmul(ps[0:48, t, :], wx[:, k, :], xa[:, k, t * 512:(t + 1) * 512],
                                       start=(k == 0), stop=(k == CD - 1))
                mm.then_inc(s_xd, 1)
                pe.wait_ge(s_parts, b + 1)
                for k in range(CD):
                    if k >= 2:
                        pe.wait_ge(s_abs, b * CD + k - 1)
                    for t in range(2):
                        mm = pe.matmul(ps[:, 2 + 2 * (k % 2) + t, :], wdt[:, k * P:(k + 1) * P],
                                       xdt[:, t * 512:(t + 1) * 512], start=True, stop=True)
                    mm.then_inc(s_dt, 1)
                pe.wait_ge(s_abs, b * CD + CD)
                for n in range(NS):
                    if n >= 4:
                        pe.wait_ge(s_bb, b * NS + n - 3)
                    for t in range(2):
                        mm = pe.matmul(ps[:, 2 * (n % 4) + t, :], sel[:, n:n + 1].to_broadcast([96, P]),
                                       parts[:, t * 512:(t + 1) * 512], start=True, stop=True)
                    mm.then_inc(s_bps, 1)
                with pe.Fori(0, CD) as k:
                    pe.wait_ge(s_bb, b * NS + NS)

                    def c_row(n, at):
                        pe.wait_ge(s_g, 1 + at)
                        for t in range(2):
                            mm = pe.matmul(ps[:, t, :], sel[:, NS + n:NS + n + 1].to_broadcast([96, P]),
                                           parts[:, t * 512:(t + 1) * 512], start=True, stop=True)
                        mm.then_inc(s_c, 1)

                    c_row(0, (b * CD + k) * NS)
                    pe.wait_ge(s_gated, 1 + b * CD + k)
                    for n in range(NS):
                        at = (b * CD + k) * NS + n
                        if n + 1 < NS:
                            c_row(n + 1, at + 1)
                        else:
                            pe.wait_ge(s_g, 1 + at + 1)
                        for t in range(2):
                            mm = pe.matmul(ps[:, 2 + t, :], ident[:, :], h[:, n % 2, t * 512:(t + 1) * 512],
                                           start=(n == 0), stop=(n == NS - 1))
                        mm.then_inc(s_y, 1)
                pe.wait_ge(s_gated, 1 + b * CD + CD)
                for j in range(TB):
                    for k in range(CD):
                        mm = pe.matmul(ps[:, j, 0:D], xa[:, k, j * P:(j + 1) * P], wout[:, k, :],
                                       start=(k == 0), stop=(k == CD - 1))
                    mm.then_inc(s_op, 1)



def moe(nc, g, layer, F, router, gate_w, up_w, down_w, hs=None, norm_w=None):
    ctx = ExitStack()
    with ctx:
        sb = lambda n, s, d=F32: ctx.enter_context(nc.sbuf_tensor(f"e{layer}_{n}", s, d))
        sem = lambda n: ctx.enter_context(nc.semaphore(f"e{layer}_{n}"))
        x, mod, ps, ident = g.x, g.mod, g.ps, g.ident
        FB = 1 if F <= 512 else 2
        FN = F // FB
        FCH = [(c * P, min(P, F - c * P)) for c in range(-(-F // P))]
        NF = len(FCH)
        FULL = F // P
        S = SLOT_TILES
        wg, wu = sb("wg", [P, EXP, KC, F]), sb("wu", [P, EXP, KC, F])
        wd = sb("wd", [P, EXP, NF, D])
        xn = sb("xn", [P, NT, D])
        nrm = norm_buffers(sb, f"e{layer}_n")
        tri, ones = sb("tri", [P, P]), sb("ones", [P, P])
        rw = sb("rw", [P, KC, EXP])
        xT = sb("xT", [P, 2, 4 * P])
        hT = sb("hT", [P, 2, NF * P])
        xin = sb("xin", [P, 2, D])
        sg, hh = sb("sg", [P, F]), sb("hh", [P, F])
        yo = sb("yo", [P, 2, D])
        zero = yo[:, 0, :]
        nwb = sb("nwb", [P, D]) if norm_w is not None else None
        cut = lambda t, a, n, m: t[:, a:a + n * m].rearrange("p (a b) -> p a b", a=n)
        lg, top = cut(sg, 0, NT, EXP), cut(sg, 128, NT, 8)
        idx = sb("idx", [P, NT, 8], U32)
        idf = sb("idf", [P, 2, NT])
        hot = sb("hot", [P, 2, NT, EXP])
        m, rank, tot, incl = (sb(n, [P, NT, EXP]) for n in ("m", "rank", "tot", "incl"))
        e8, row16 = sb("e8", [P, EXP]), sb("row16", [P, NT])
        row40 = sb("row40", [P, S])
        low8 = sb("low8", [P, EXP, EXP])
        one16 = sb("one16", [P, NT])
        cmp, tmp8, cmp_tile = cut(sg, 256, EXP, NT), cut(sg, 384, EXP, EXP), cut(hh, 0, S, EXP)
        cnt, first8 = sb("cnt", [P, EXP]), sb("first8", [P, EXP])
        texp_f, texp = sb("texp_f", [P, S]), sb("texp", [P, S], I32)
        posf, pos = sb("posf", [P, 2, NT]), sb("pos", [P, 2, NT], U32)
        prob, ex, den = sb("prob", [P, 2, NT]), sb("ex", [P, NT]), sb("den", [P, NT])
        GR = 4
        gat = wg[:, 0, :, :].rearrange("p a b -> p (a b)")[:, 0:D * 4].rearrange("p (r d) -> p r d", d=D)
        gat2 = wg[:, 1, :, :].rearrange("p a b -> p (a b)")[:, 0:D * 4].rearrange("p (r d) -> p r d", d=D)
        slots = nc.dram_tensor(f"e{layer}_slots", [S * P, D], F32, kind="Internal").ap()
        outs = nc.dram_tensor(f"e{layer}_outs", [S * P, D], F32, kind="Internal").ap()

        s_in, s_w, s_z, s_zm = sem("in"), sem("w"), sem("z"), sem("zm")
        s_own, s_var, s_sd, s_xn = sem("own"), sem("var"), sem("sd"), sem("xn")
        s_tr, s_xT, s_lg = sem("tr"), sem("xT"), sem("lg")
        s_ex, s_exd, s_m, s_rank = sem("ex"), sem("exd"), sem("m"), sem("rank")
        s_texp, s_pos, s_sc = sem("texp"), sem("pos"), sem("sc")
        s_xin = [sem("xin0"), sem("xin1")]
        s_xtp, s_xts, s_gu, s_sg, s_h = sem("xtp"), sem("xts"), sem("gu"), sem("sg"), sem("h")
        s_thp, s_hts, s_y, s_ys = sem("thp"), sem("hts"), sem("y"), sem("ys")
        s_st = [sem("st0"), sem("st1")]
        s_ga = [sem(f"ga{r}") for r in range(GR)]
        s_comb, s_res = sem("comb"), sem("res")
        block = ctx.enter_context(nc.Block())
        NCONST = 7 + (norm_w is not None)

        @block.sync
        def _(sp):
            consts = [(tri[:, :], g.d["tri"]), (ones[:, :], g.d["ones"]), (e8[:, :], g.d["e8"]), (row16[:, :], g.d["row16"]),
                      (row40[:, :], g.d["row40"]), (low8[:, :, :], g.d["low8"].rearrange("p (a b) -> p a b", a=EXP)),
                      (rw[:, :, :], router.rearrange("(k p) e -> p k e", p=P))]
            if norm_w is not None:
                consts.append((nwb[:, :], norm_w.rearrange("(a n) -> a n", a=1).to_broadcast([P, D])))
            for dst, src in consts:
                sp.dma_start(dst, src).then_inc(s_in, 16)
            sp.wait_ge(s_zm, 1)
            sp.dma_start(slots.rearrange("(t p) d -> p t d", p=P), over(zero, S)).then_inc(s_z, 16)
            for e in range(EXP):
                sp.dma_start(wg[:, e, :, :], gate_w[e].rearrange("(k p) f -> p k f", p=P)).then_inc(s_w, 16)
                sp.dma_start(wu[:, e, :, :], up_w[e].rearrange("(k p) f -> p k f", p=P)).then_inc(s_w, 16)
                sp.dma_start(wd[:, e, 0:FULL, :], down_w[e, 0:FULL * P].rearrange("(c p) d -> p c d", p=P)).then_inc(s_w, 16)
                if FULL < NF:
                    sp.dma_start(wd[0:F - FULL * P, e, FULL, :], down_w[e, FULL * P:F]).then_inc(s_w, 16)
            sp.wait_ge(s_sc, 16 * 2 * NT)

            def load_pair(i2):
                for q in range(2):
                    i = i2 * 2 + q
                    after(sp, s_xtp, i2 * 2)
                    sp.dma_start(xin[:, q, :], slots[ds(i * P, P), :]).then_inc(s_xin[q], 16)

            load_pair(0)
            with sp.Fori(1, S // 2) as i2:
                load_pair(i2)

        WLOADS = EXP * (3 + (FULL < NF)) * 16

        @block.gpsimd
        def _(pool):
            pool.wait_ge(s_z, 16)
            pool.wait_ge(s_pos, 1)
            for j in range(NT):
                for k in range(2):
                    pool.indirect_dma_start(slots[:, :], bass.IndirectOffsetOnAxis(ap=pos[:, k, j:j + 1], axis=0),
                                            xn[:, j, :], None).then_inc(s_sc, 16)
            with pool.Fori(0, S // 2) as i2:
                for q in range(2):
                    pool.wait_ge(s_ys, i2 * 2 + q + 1)
                    pool.dma_start(outs[ds((i2 * 2 + q) * P, P), :], yo[:, q, :]).then_inc(s_st[q], 16)
            for q in range(2):
                pool.wait_ge(s_st[q], 16 * (S // 2))
            for j in range(NT):
                r = j % GR
                if j >= GR:
                    pool.wait_ge(s_comb, j - GR + 1)
                for k, dst in enumerate((gat, gat2)):
                    pool.indirect_dma_start(dst[:, r, :], None, outs[:, :],
                                            bass.IndirectOffsetOnAxis(ap=pos[:, k, j:j + 1], axis=0)).then_inc(s_ga[r], 16)

        @block.scalar
        def _(act):
            act_sqrt(act, nrm, s_var, s_sd, 1)
            for r in range(NT // 2):
                act.wait_ge(s_tr, r + 1)
                if r >= 2:
                    act.wait_ge(s_lg, 2 * (r - 1))
                act.activation(xT[:, r % 2, :], ps[:, r % 2, :], ACT.Copy).then_inc(s_xT, 1)
            act.wait_ge(s_exd, 1)
            act.activation(ex[:, :], ex[:, :], ACT.Exp).then_inc(s_ex, 1)

            def tile_pair(i2):
                for q in range(2):
                    i = i2 * 2 + q
                    act.wait_ge(s_gu, i + 1)
                    after(act, s_h, i)
                    act.activation(sg[:, :].rearrange("p (a n) -> p a n", a=FB), ps[:, 0:FB, 0:FN], ACT.Silu).then_inc(s_sg, 1)
                    act.wait_ge(s_thp, i + 1)
                    half = NF // 2
                    for a in range(2):
                        n = half if a == 0 else NF - half
                        act_i = act.activation(hT[:, q, a * half * P:(a * half + n) * P], ps[:, 4 + a, 0:n * P], ACT.Copy)
                    act_i.then_inc(s_hts, 1)

            tile_pair(0)
            with act.Fori(1, S // 2) as i2:
                tile_pair(i2)

        @block.tensor
        def _(pe):
            pe.wait_ge(s_xn, 1)
            pe.wait_ge(s_in, 16 * NCONST)
            def logits(r):
                for t in range(2):
                    j = 2 * r + t
                    for k in range(KC):
                        mm = pe.matmul(ps[:, 7, j * EXP:(j + 1) * EXP], xT[:, r % 2, (2 * t + k) * P:(2 * t + k + 1) * P],
                                       rw[:, k, :], start=(k == 0), stop=(k == KC - 1))
                    mm.then_inc(s_lg, 1)
            for r in range(NT // 2):
                if r >= 2:
                    pe.wait_ge(s_xT, r - 1)
                for t in range(2):
                    for k in range(KC):
                        tr = pe.transpose(ps[:, r % 2, (2 * t + k) * P:(2 * t + k + 1) * P],
                                          xn[:, 2 * r + t, k * P:(k + 1) * P], ident[:, :])
                tr.then_inc(s_tr, 1)
                if r >= 1:
                    pe.wait_ge(s_xT, r)
                    logits(r - 1)
            pe.wait_ge(s_xT, NT // 2)
            logits(NT // 2 - 1)
            pe.wait_ge(s_m, 1)
            pe.matmul(ps[:, 2, 0:P], tri[:, :], m[:, :, :].rearrange("p a b -> p (a b)"), start=True, stop=True)
            pe.matmul(ps[:, 3, 0:P], ones[:, :], m[:, :, :].rearrange("p a b -> p (a b)"), start=True, stop=True).then_inc(s_rank, 1)
            pe.wait_ge(s_texp, 1)
            pe.wait_ge(s_w, WLOADS)

            def turn_x(i, q, loads):
                pe.wait_ge(s_xin[q], 16 * loads)
                after(pe, s_xts, i)
                for k in range(KC):
                    tr = pe.transpose(ps[:, 7, k * P:(k + 1) * P], xin[:, q, k * P:(k + 1) * P], ident[:, :])
                tr.then_inc(s_xtp, 1)

            def gate_up(i, q):
                e = pe.value_load(texp[0:1, ds(i)], min_val=0, max_val=EXP - 1)
                pe.wait_ge(s_xts, i + 1)
                after(pe, s_h, i)
                for w, b0 in ((wg, 0), (wu, 2)):
                    for k in range(KC):
                        for a in range(FB):
                            mm = pe.matmul(ps[:, b0 + a, 0:FN], xT[:, q, k * P:(k + 1) * P],
                                           w[:, ds(e), k, a * FN:(a + 1) * FN].rearrange("p a n -> p (a n)"),
                                           start=(k == 0), stop=(k == KC - 1))
                mm.then_inc(s_gu, 1)

            def turn_h(i):
                pe.wait_ge(s_h, i + 1)
                after(pe, s_hts, i)
                half = NF // 2
                for c, (f0, n) in enumerate(FCH):
                    a, col = (0, c) if c < half else (1, c - half)
                    tr = pe.transpose(ps[0:n, 4 + a, col * P:(col + 1) * P], hh[:, f0:f0 + n], ident[:, :])
                tr.then_inc(s_thp, 1)

            def down(i, q, yfree):
                e = pe.value_load(texp[0:1, ds(i)], min_val=0, max_val=EXP - 1)
                pe.wait_ge(s_hts, i + 1)
                after(pe, s_ys, yfree)
                for c, (f0, n) in enumerate(FCH):
                    mm = pe.matmul(ps[:, 6, 0:D], hT[0:n, q, c * P:(c + 1) * P],
                                   wd[0:n, ds(e), c, :].rearrange("p a n -> p (a n)"), start=(c == 0), stop=(c == NF - 1))
                mm.then_inc(s_y, 1)

            turn_x(0, 0, 1)
            gate_up(0, 0)
            turn_x(1, 1, 1)
            turn_h(0)

            def tile_pair(i2):
                for q in (1, 0):
                    i = i2 * 2 + (1 if q else 2)
                    gate_up(i, q)
                    down(i - 1, 1 - q, i - 1)
                    turn_x(i + 1, 1 - q, i2 + 2)
                    turn_h(i)

            tile_pair(0)
            with pe.Fori(1, S // 2 - 1) as i2:
                tile_pair(i2)
            gate_up(S - 1, 1)
            down(S - 2, 0, S - 2)
            turn_h(S - 1)
            down(S - 1, 1, S - 1)

        @block.vector
        def _(dve):
            own = Own(dve, s_own)
            dve.memset(zero, 0.0).then_inc(s_zm, 1)
            own(dve.memset(one16[:, :], 1.0))
            st, mean, var, sd, rstd, t = nrm
            if hs is None:
                dve_rstd(dve, own, x, nrm, s_var, s_sd, 1, False)
                for j in range(NT):
                    own.mark(dve.tensor_scalar(xn[:, j, :], x[:, j, :], mean[:, j:j + 1], rstd[:, j:j + 1],
                                               ALU.subtract, ALU.mult))
                own.wait()
                for b in range(B):
                    v = xn[:, b * TB:(b + 1) * TB, :]
                    own(dve.tensor_tensor(v, v, over(mod[:, b, CB * D:(CB + 1) * D], TB), ALU.mult))
                    ins = dve.tensor_tensor(v, v, over(mod[:, b, SB * D:(SB + 1) * D], TB), ALU.add)
                ins.then_inc(s_xn, 1)
            else:
                dve_rstd(dve, own, hs, nrm, s_var, s_sd, 1, True)
                dve.wait_ge(s_in, 16 * NCONST)
                own.wait()
                for j in range(NT):
                    ins = dve.scalar_tensor_tensor(xn[:, j, :], hs[:, j, :], rstd[:, j:j + 1], nwb[:, :], ALU.mult, ALU.mult)
                ins.then_inc(s_xn, 1)
            dve.wait_ge(s_in, 16 * NCONST)
            dve.wait_ge(s_lg, NT)
            own(dve.tensor_copy(lg, ps[:, 7, 0:P].rearrange("p (a b) -> p a b", a=NT)))
            for j in range(NT):
                own.mark(dve.max(top[:, j, :], lg[:, j, :]))
            own.wait()
            for j in range(NT):
                own.mark(dve.max_index(idx[:, j, :], top[:, j, :], lg[:, j, :]))
            dve.tensor_tensor(ex[:, :], top[:, :, 1], top[:, :, 0], ALU.subtract).then_inc(s_exd, 1)
            own.wait()
            own(dve.tensor_copy(idf[:, :, :], idx[:, :, 0:2].rearrange("p j k -> p k j")))
            for k in range(2):
                own.mark(dve.tensor_tensor(hot[:, k, :, :], over(e8[:, :], NT),
                                           idf[:, k, :].rearrange("p (j a) -> p j a", a=1).to_broadcast([P, NT, EXP]), ALU.is_equal))
            own.wait()
            dve.tensor_tensor(m[:, :, :], hot[:, 0, :, :], hot[:, 1, :, :], ALU.add).then_inc(s_m, 1)
            dve.wait_ge(s_ex, 1)
            own(dve.tensor_scalar(den[:, :], ex[:, :], 1.0, None, ALU.add))
            own(dve.reciprocal(prob[:, 0, :], den[:, :]))
            own(dve.tensor_tensor(prob[:, 1, :], prob[:, 0, :], ex[:, :], ALU.mult))
            dve.wait_ge(s_rank, 1)
            own.mark(dve.tensor_copy(rank[:, :, :], ps[:, 2, 0:P].rearrange("p (a b) -> p a b", a=NT)))
            own(dve.tensor_copy(tot[:, :, :], ps[:, 3, 0:P].rearrange("p (a b) -> p a b", a=NT)))
            for e in range(EXP):
                own.mark(dve.tensor_tensor_scan(incl[:, :, e], one16[:, :], tot[:, :, e], 0.0, ALU.mult, ALU.add))
            own.wait()
            own(dve.tensor_tensor(tot[:, :, :], incl[:, :, :], tot[:, :, :], ALU.subtract))
            own(dve.tensor_tensor(rank[:, :, :], rank[:, :, :], tot[:, :, :], ALU.add))
            own(dve.tensor_tensor(cmp, incl[:, NT - 1, :].rearrange("p (e a) -> p e a", a=1).to_broadcast([P, EXP, NT]),
                                  over(row16[:, :], EXP), ALU.is_gt))
            own(dve.tensor_reduce(cnt[:, :], cmp, AX_X, ALU.add))
            own(dve.tensor_scalar(cnt[:, :], cnt[:, :], 1.0, None, ALU.add))
            own(dve.tensor_tensor(tmp8, low8[:, :, :], over(cnt[:, :], EXP), ALU.mult))
            own(dve.tensor_reduce(first8[:, :], tmp8, AX_X, ALU.add))
            own(dve.tensor_tensor(cmp_tile, row40[:, :].rearrange("p (s a) -> p s a", a=1).to_broadcast([P, S, EXP]),
                                  over(first8[:, :], S), ALU.is_ge))
            own(dve.tensor_reduce(texp_f[:, :], cmp_tile, AX_X, ALU.add))
            own(dve.tensor_scalar(texp_f[:, :], texp_f[:, :], -1.0, None, ALU.add))
            dve.tensor_copy(texp[:, :], texp_f[:, :]).then_inc(s_texp, 1)
            own(dve.tensor_scalar(first8[:, :], first8[:, :], float(P), None, ALU.mult))
            own(dve.tensor_tensor(rank[:, :, :], rank[:, :, :], over(first8[:, :], NT), ALU.add))
            for k in range(2):
                own.mark(dve.tensor_tensor(hot[:, k, :, :], hot[:, k, :, :], rank[:, :, :], ALU.mult))
            own.wait()
            for k in range(2):
                own.mark(dve.tensor_reduce(posf[:, k, :], hot[:, k, :, :], AX_X, ALU.add))
            own.wait()
            dve.tensor_copy(pos[:, :, :], posf[:, :, :]).then_inc(s_pos, 1)

            def take_x(i, q):
                dve.wait_ge(s_xtp, i + 1)
                dve.tensor_copy(xT[:, q, 0:D], ps[:, 7, 0:D]).then_inc(s_xts, 1)

            def take_y(i, q, stores):
                dve.wait_ge(s_y, i + 1)
                after(dve, s_st[q], 16 * stores)
                dve.tensor_copy(yo[:, q, :], ps[:, 6, 0:D]).then_inc(s_ys, 1)

            def hidden(i):
                dve.wait_ge(s_sg, i + 1)
                after(dve, s_thp, i)
                dve.tensor_tensor(hh[:, :].rearrange("p (a n) -> p a n", a=FB), sg[:, :].rearrange("p (a n) -> p a n", a=FB),
                                  ps[:, 2:2 + FB, 0:FN], ALU.mult).then_inc(s_h, 1)

            take_x(0, 0)
            hidden(0)
            take_x(1, 1)

            def tile_pair(i2):
                for q in (1, 0):
                    i = i2 * 2 + (1 if q else 2)
                    hidden(i)
                    take_y(i - 1, 1 - q, i2)
                    take_x(i + 1, 1 - q)

            tile_pair(0)
            with dve.Fori(1, S // 2 - 1) as i2:
                tile_pair(i2)
            hidden(S - 1)
            take_y(S - 2, 0, S // 2 - 1)
            take_y(S - 1, 1, S // 2 - 1)
            for j in range(NT):
                r = j % GR
                dve.wait_ge(s_ga[r], 32 * (j // GR + 1))
                own(dve.tensor_scalar(gat[:, r, :], gat[:, r, :], prob[:, 0, j:j + 1], None, ALU.mult))
                own(dve.scalar_tensor_tensor(gat2[:, r, :], gat2[:, r, :], prob[:, 1, j:j + 1], gat[:, r, :], ALU.mult, ALU.add))
                if hs is not None:
                    own(dve.tensor_tensor(gat2[:, r, :], gat2[:, r, :], hs[:, j, :], ALU.add))
                own(dve.tensor_tensor(gat2[:, r, :], gat2[:, r, :], mod[:, j // TB, GB * D:(GB + 1) * D], ALU.mult))
                dve.tensor_tensor(x[:, j, :], x[:, j, :], gat2[:, r, :], ALU.add).then_inc(s_comb, 1)



def attn1(nc, g, wq, wk, wv, fc_w, fc_b):
    ctx = ExitStack()
    with ctx:
        sb = lambda n, s, d=F32: ctx.enter_context(nc.sbuf_tensor(f"a1_{n}", s, d))
        sem = lambda n: ctx.enter_context(nc.semaphore(f"a1_{n}"))
        x, mod, ps, ident = g.x, g.mod, g.ps, g.ident
        SCALE = 1.0 / float(np.sqrt(np.float32(D)))
        w = {n: sb("w" + n, [P, KC, AH * D]) for n in "qkv"}
        fw, fb, ones = sb("fw", [P, KC, D]), sb("fb", [1, D]), sb("ones", [1, P])
        nrm = norm_buffers(sb, "a1_n")
        xn, hT = sb("xn", [P, TB, D]), sb("hT", [P, KC, L])
        qT, kT, v = sb("qT", [P, 2, KC, L]), sb("kT", [P, 2, KC, L]), sb("v", [P, 2, TB, D])
        e = sb("e", [P, 2, L])
        vs = sb("vs", [P, 2, D])
        mx, nb, sm, rc = (sb(n, [P, TB]) for n in ("mx", "nb", "sm", "rc"))
        aT = sb("aT", [P, KC, L])
        t1 = sb("t1", [P, 2, D])
        s_in, s_own, s_var, s_sd, s_xn = sem("in"), sem("own"), sem("var"), sem("sd"), sem("xn")
        s_tr, s_hT = sem("tr"), sem("hT")
        s_unit, s_free = sem("unit"), sem("free")
        s_nb, s_e, s_vs, s_av = sem("nb"), sem("e"), sem("vs"), sem("av")
        s_aT, s_res = sem("aT"), sem("res")
        block = ctx.enter_context(nc.Block())
        PROJ = 6
        PER_HEAD = PROJ + TB
        UNITS = AH * PER_HEAD

        def pair(i):
            return flat(ps[:, 2 * i:2 * i + 2, :])

        def order():
            todo = [("proj", 0, i) for i in range(PROJ)]
            for h in range(AH):
                for m in range(TB):
                    todo.append(("score", h, m))
                    if m == TB // 2 and h + 1 < AH:
                        todo += [("proj", h + 1, i) for i in range(PROJ)]
            return todo

        todo = order()
        assert len(todo) == UNITS and UNITS % 2 == 0
        read_at = {h: 1 + max(n for n, (kind, hh, _) in enumerate(todo) if kind == "proj" and hh == h) for h in range(AH)}

        @block.sync
        def _(sp):
            for n, src in (("q", wq), ("k", wk), ("v", wv)):
                sp.dma_start(w[n][:, :, :], src.rearrange("(k p) n -> p k n", p=P)).then_inc(s_in, 16)
            sp.dma_start(fw[:, :, :], fc_w.rearrange("(k p) n -> p k n", p=P)).then_inc(s_in, 16)
            sp.dma_start(fb[:, :], fc_b).then_inc(s_in, 16)
            sp.dma_start(ones[:, :], g.d["ones"][0:1, :]).then_inc(s_in, 16)
            sp.wait_ge(s_in, 96)

        @block.tensor
        def _(pe):
            pe.sem_inc(s_av, 1)
            pe.wait_ge(s_in, 96)

            def project(b, n, h, i):
                unit_free(b, n)
                s, o = h % 2, n % 2
                if i < 4:
                    wt = w["q" if i < 2 else "k"]
                    for t in range(2):
                        for k in range(KC):
                            mm = pe.matmul(ps[:, 2 * o + t, :], wt[:, k, h * D + (i % 2) * P:h * D + (i % 2 + 1) * P],
                                           hT[:, k, t * 512:(t + 1) * 512], start=(k == 0), stop=(k == KC - 1))
                else:
                    for t in range(4):
                        j = (i - 4) * 4 + t
                        for k in range(KC):
                            mm = pe.matmul(ps[:, 2 * o + t // 2, (t % 2) * D:(t % 2 + 1) * D], hT[:, k, j * P:(j + 1) * P],
                                           w["v"][:, k, h * D:(h + 1) * D], start=(k == 0), stop=(k == KC - 1))
                mm.then_inc(s_unit, 1)

            def unit_free(b, n):
                if n >= 2:
                    pe.wait_ge(s_free, b * UNITS + n - 1)

            def scores(b, n, h, m):
                unit_free(b, n)
                if m == 0:
                    pe.wait_ge(s_free, b * UNITS + read_at[h])
                for t in range(2):
                    for k in range(KC):
                        mm = pe.matmul(ps[:, 2 * (n % 2) + t, :], kT[:, h % 2, k, m * P:(m + 1) * P],
                                       qT[:, h % 2, k, t * 512:(t + 1) * 512], start=(k == 0), stop=(k == KC - 1))
                mm.then_inc(s_unit, 1)

            def values(b, h, m):
                at = (b * AH + h) * TB + m
                pe.wait_ge(s_vs, at + 1)
                for c in range(KC):
                    for t in range(2):
                        mm = pe.matmul(ps[:, 4 + 2 * c + t, :], vs[:, m % 2, c * P:(c + 1) * P], e[:, m % 2, t * 512:(t + 1) * 512],
                                       start=(h == 0 and m == 0), stop=(h == AH - 1 and m == TB - 1))
                mm.then_inc(s_av, 1)

            with pe.Fori(0, B) as b:
                pe.wait_ge(s_xn, b + 1)
                pe.wait_ge(s_aT, 1 + 2 * b)
                for q in range(4):
                    for j in range(4):
                        tr = pe.transpose(ps[:, 4 + q, j * P:(j + 1) * P],
                                          xn[:, 4 * (q % 2) + j, (q // 2) * P:(q // 2 + 1) * P], ident[:, :])
                    tr.then_inc(s_tr, 1)
                pe.wait_ge(s_hT, b * 4 + 4)
                pe.wait_ge(s_res, 1 + b * TB)
                late = None
                for n, (kind, h, i) in enumerate(todo):
                    if kind == "proj":
                        project(b, n, h, i)
                    else:
                        scores(b, n, h, i)
                        if late is not None:
                            values(b, *late)
                        late = (h, i)
                values(b, *late)
                pe.wait_ge(s_aT, 1 + 2 * b + 2)
                pe.wait_ge(s_free, b * UNITS + UNITS)
                for j in range(TB):
                    o = ps[:, j // 2, (j % 2) * D:(j % 2 + 1) * D]
                    for k in range(KC):
                        pe.matmul(o, aT[:, k, j * P:(j + 1) * P], fw[:, k, :], start=(k == 0), stop=False)
                    mm = pe.matmul(o, ones[:, :], fb[:, :], start=False, stop=True)
                mm.then_inc(s_unit, 1)

        @block.scalar
        def _(act):
            act.sem_inc(s_aT, 1)
            act_sqrt(act, nrm, s_var, s_sd, 1)
            with act.Fori(0, B) as b:
                for q in range(4):
                    act.wait_ge(s_tr, b * 4 + q + 1)
                    act.activation(hT[:, q // 2, (q % 2) * 512:(q % 2) * 512 + 512], ps[:, 4 + q, :], ACT.Copy).then_inc(s_hT, 1)
                for n, (kind, h, i) in enumerate(todo):
                    act.wait_ge(s_unit, b * (UNITS + 1) + n + 1)
                    if kind == "proj":
                        if h >= 2 and i == 0:
                            act.wait_ge(s_av, 1 + (b * AH + h - 1) * TB)
                        if h < 2 and i == 0:
                            act.wait_ge(s_av, 1 + b * AH * TB)
                        dst = (qT[:, h % 2, i, :] if i < 2 else kT[:, h % 2, i - 2, :] if i < 4 else
                               flat(v[:, h % 2, (i - 4) * 4:(i - 4) * 4 + 4, :]))
                        act.activation(dst, pair(n % 2), ACT.Copy).then_inc(s_free, 1)
                    else:
                        at = (b * AH + h) * TB + i
                        act.wait_ge(s_nb, at + 1)
                        if i >= 2 or h >= 1:
                            act.wait_ge(s_av, 1 + at - 1)
                        act.activation(e[:, i % 2, :], pair(n % 2), ACT.Exp, bias=nb[:, i:i + 1], scale=SCALE,
                                       accum_out=sm[:, i:i + 1]).then_inc(s_free, 1)
                for k in range(KC):
                    act.wait_ge(s_av, 1 + (b + 1) * AH * TB)
                    act.activation(aT[:, k, :], pair(2 + k), ACT.Copy).then_inc(s_aT, 1)

        @block.vector
        def _(dve):
            own = Own(dve, s_own)
            dve.sem_inc(s_res, 1)
            dve_rstd(dve, own, x, nrm, s_var, s_sd, 1, False)
            st, mean, var, sd, rstd, t = nrm
            with dve.Fori(0, B) as b, own.turn(b, B, TB + 1 + AH * TB * 2 + TB):
                for j in range(TB):
                    c = b * TB + j
                    own.mark(dve.tensor_scalar(xn[:, j, :], flat(x[:, ds(c), :]), mean[:, ds(c)], rstd[:, ds(c)],
                                               ALU.subtract, ALU.mult))
                own.wait()
                own(dve.tensor_tensor(xn[:, :, :], xn[:, :, :], over(modvec(mod, b, CA), TB), ALU.mult))
                dve.tensor_tensor(xn[:, :, :], xn[:, :, :], over(modvec(mod, b, SA), TB), ALU.add).then_inc(s_xn, 1)
                late = None

                def value_rows(n, h, m):
                    at = (b * AH + h) * TB + m
                    dve.wait_ge(s_free, b * UNITS + n + 1)
                    own(dve.reciprocal(rc[:, m:m + 1], sm[:, m:m + 1]))
                    if at_least_two[(h, m)]:
                        dve.wait_ge(s_av, 1 + at - 1)
                    dve.tensor_scalar(vs[:, m % 2, :], v[:, h % 2, m, :], rc[:, m:m + 1], 1.0 / AH,
                                      ALU.mult, ALU.mult).then_inc(s_vs, 1)

                at_least_two = {(h, m): h > 0 or m >= 2 for h in range(AH) for m in range(TB)}
                for n, (kind, h, i) in enumerate(todo):
                    if kind == "score":
                        dve.wait_ge(s_unit, b * (UNITS + 1) + n + 1)
                        own(dve.reduce_max(mx[:, i:i + 1], pair(n % 2), AX_X))
                        dve.tensor_scalar(nb[:, i:i + 1], mx[:, i:i + 1], -SCALE, None, ALU.mult).then_inc(s_nb, 1)
                        if late is not None:
                            value_rows(*late)
                        late = (n, h, i)
                value_rows(*late)
                for j in range(TB):
                    dve.wait_ge(s_unit, (b + 1) * (UNITS + 1))
                    if j >= 2:
                        dve.wait_ge(s_res, 1 + b * TB + j - 1)
                    xj = flat(x[:, ds(b * TB + j), :])
                    own(dve.tensor_tensor(t1[:, j % 2, :], ps[:, j // 2, (j % 2) * D:(j % 2 + 1) * D], modvec(mod, b, GA), ALU.mult))
                    dve.tensor_tensor(xj, xj, t1[:, j % 2, :], ALU.add).then_inc(s_res, 1)
                dve.wait_ge(s_res, 1 + b * TB + TB)



def attn2(nc, g, hs, norm_w, wq, wk, wv, wo):
    ctx = ExitStack()
    with ctx:
        sb = lambda n, s, d=F32: ctx.enter_context(nc.sbuf_tensor(f"a2_{n}", s, d))
        sem = lambda n: ctx.enter_context(nc.semaphore(f"a2_{n}"))
        x, mod, ps, ident = g.x, g.mod, g.ps, g.ident
        SCALE = 1.0 / float(np.sqrt(HD))
        nrm = norm_buffers(sb, "a2_n")
        nwb = sb("nwb", [P, D])
        xn, hT = sb("xn", [P, TB, D]), sb("hT", [P, KC, L])
        wq_s, wk_s, wv_s = sb("wq", [P, KC, REP * HD]), sb("wk", [P, KC, HD]), sb("wv", [P, KC, HD])
        wo_s = sb("wo", [P, H, D])
        cos, sin = sb("cos", [P, L]), sb("sin", [P, L])
        mask_f, mask, ident_b = sb("mask_f", [P, P]), sb("mask", [P, P], BF16), sb("ident_b", [P, P], BF16)
        qT, kT, v = sb("qT", [P, REP, L]), sb("kT", [P, L]), sb("v", [P, TB, HD])
        e = sb("e", [P, 2, REP, L])
        r1, r2 = e[:, 0, 0:2, :], e[:, 0, 2:4, :]
        eT = sb("eT", [P, 2, REP * P])
        ao = sb("ao", [P, 2, REP, P])
        mx, nb, sm, rc = (sb(n, [P, 2 * REP]) for n in ("mx", "nb", "sm", "rc"))
        names = ("in", "own", "var", "sd", "xn", "tr", "hT", "cst", "unit", "w", "rot", "rope", "v", "nb", "e", "en",
                 "tp", "eT", "o", "ao", "wo", "hs")
        s = {n: sem(n) for n in names}
        block = ctx.enter_context(nc.Block())
        NPROJ = REP + 1
        UNITS = NPROJ + 1 + REP * TB
        BLOCKS = TB * (TB + 1) // 2

        def pair(i, w=L, p=slice(0, P)):
            return flat(ps[p, 2 * i:2 * i + 2, :])[:, 0:w]

        @block.sync
        def _(sp):
            loads = [(nwb[:, :], norm_w.rearrange("(a n) -> a n", a=1).to_broadcast([P, D])),
                     (wo_s[:, :, :], wo.rearrange("(h p) d -> p h d", p=P)), (cos[:, :], g.d["cos"]), (sin[:, :], g.d["sin"]),
                     (mask_f[:, :], g.d["mask"])]
            for dst, src in loads:
                sp.dma_start(dst, src).then_inc(s["in"], 16)
            with sp.Fori(0, B) as b:
                with sp.Fori(0, KV) as kv:
                    it = b * KV + kv
                    sp.wait_ge(s["v"], 1 + it)
                    sp.dma_start(wq_s[:, :, :], wq.rearrange("(k p) n -> p k n", p=P)[:, :, ds(kv * (REP * HD), REP * HD)]).then_inc(s["w"], 16)
                    sp.dma_start(wk_s[:, :, :], wk.rearrange("(k p) n -> p k n", p=P)[:, :, ds(kv * HD, HD)]).then_inc(s["w"], 16)
                    sp.dma_start(wv_s[:, :, :], wv.rearrange("(k p) n -> p k n", p=P)[:, :, ds(kv * HD, HD)]).then_inc(s["w"], 16)

        @block.vector
        def _(dve):
            own = Own(dve, s["own"])
            dve.sem_inc(s["hs"], 1)
            st, mean, var, sd, rstd, t = nrm
            dve_rstd(dve, own, x, nrm, s["var"], s["sd"], 1, False)
            for j in range(NT):
                own.mark(dve.tensor_scalar(hs[:, j, :], x[:, j, :], mean[:, j:j + 1], rstd[:, j:j + 1], ALU.subtract, ALU.mult))
            own.wait()
            for b in range(B):
                h = hs[:, b * TB:(b + 1) * TB, :]
                own(dve.tensor_tensor(h, h, over(mod[:, b, CB * D:(CB + 1) * D], TB), ALU.mult))
                own(dve.tensor_tensor(h, h, over(mod[:, b, SB * D:(SB + 1) * D], TB), ALU.add))
            dve_rstd(dve, own, hs, nrm, s["var"], s["sd"], 2, True)
            dve.wait_ge(s["in"], 80)
            dve.tensor_copy(mask[:, :], mask_f[:, :])
            dve.tensor_copy(ident_b[:, :], ident[:, :]).then_inc(s["cst"], 1)
            with dve.Fori(0, B) as b, own.turn(b, B, KV * REP * TB * 2):
                for j in range(TB):
                    c = b * TB + j
                    ins = dve.scalar_tensor_tensor(xn[:, j, :], flat(hs[:, ds(c), :]), rstd[:, ds(c)], nwb[:, :], ALU.mult, ALU.mult)
                ins.then_inc(s["xn"], 1)
                with dve.Fori(0, KV) as kv, own.turn(kv, KV, REP * TB * 2):
                    it = b * KV + kv
                    for i in range(NPROJ):
                        dve.wait_ge(s["unit"], it * UNITS + i + 1)
                        if i >= 2:
                            dve.wait_ge(s["rope"], it * NPROJ + i - 1)
                        dve.tensor_tensor(r1[:, i % 2, :], pair(i % 2), cos[:, :], ALU.mult)
                        dve.tensor_tensor(r2[0:64, i % 2, :], pair(i % 2, L, slice(64, P)), sin[64:P, :], ALU.mult)
                        dve.tensor_tensor(r2[64:P, i % 2, :], pair(i % 2, L, slice(0, 64)), sin[0:64, :],
                                          ALU.mult).then_inc(s["rot"], 1)
                    late = None

                    def normal(i, h, at):
                        q = (i % 2) * REP + h
                        dve.wait_ge(s["e"], at + 1)
                        own(dve.reciprocal(rc[:, q:q + 1], sm[:, q:q + 1]))
                        dve.tensor_scalar(e[:, i % 2, h, 0:(i + 1) * P], e[:, i % 2, h, 0:(i + 1) * P], rc[:, q:q + 1], None,
                                          ALU.mult).then_inc(s["en"], 1)

                    def residual(i):
                        hj = flat(hs[:, ds(b * TB + i), :])
                        dve.wait_ge(s["wo"], it * TB + i + 1)
                        dve.tensor_tensor(hj, ps[:, 7, 0:D], hj, ALU.add).then_inc(s["hs"], 1)

                    for i in range(TB):
                        for h in range(REP):
                            n = NPROJ + 1 + i * REP + h
                            q = (i % 2) * REP + h
                            dve.wait_ge(s["unit"], it * UNITS + n + 1)
                            own(dve.reduce_max(mx[:, q:q + 1], pair(n % 2, (i + 1) * P), AX_X))
                            dve.tensor_scalar(nb[:, q:q + 1], mx[:, q:q + 1], -SCALE, None, ALU.mult).then_inc(s["nb"], 1)
                            if late is not None:
                                normal(*late)
                            late = (i, h, it * REP * TB + i * REP + h)
                        if i >= 2:
                            residual(i - 2)
                    normal(*late)
                    residual(TB - 2)
                    residual(TB - 1)

        @block.gpsimd
        def _(pool):
            with pool.Fori(0, B * KV) as it:
                for i in range(NPROJ):
                    pool.wait_ge(s["rot"], it * NPROJ + i + 1)
                    pool.tensor_tensor(qT[:, i, :] if i < REP else kT[:, :], r1[:, i % 2, :], r2[:, i % 2, :], ALU.add).then_inc(s["rope"], 1)

        @block.scalar
        def _(act):
            act.sem_inc(s["v"], 1)
            act_sqrt(act, nrm, s["var"], s["sd"], 1)
            act_sqrt(act, nrm, s["var"], s["sd"], 2)
            with act.Fori(0, B) as b:
                for q in range(4):
                    act.wait_ge(s["tr"], b * 4 + q + 1)
                    act.activation(hT[:, q // 2, (q % 2) * 512:(q % 2) * 512 + 512], ps[:, q, :], ACT.Copy).then_inc(s["hT"], 1)
                with act.Fori(0, KV) as kv:
                    it = b * KV + kv
                    act.wait_ge(s["unit"], it * UNITS + NPROJ + 1)
                    act.activation(flat(v[:, :, :]), pair(NPROJ % 2), ACT.Copy).then_inc(s["v"], 1)

                    def exps(i, h):
                        n = NPROJ + 1 + i * REP + h
                        q, at = (i % 2) * REP + h, it * REP * TB + i * REP + h
                        act.wait_ge(s["nb"], at + 1)
                        if h == 0 and i >= 2:
                            act.wait_ge(s["tp"], it * BLOCKS + i * (i - 1) // 2)
                        act.activation(e[:, i % 2, h, 0:(i + 1) * P], pair(n % 2, (i + 1) * P), ACT.Exp, bias=nb[:, q:q + 1],
                                       scale=SCALE, accum_out=sm[:, q:q + 1]).then_inc(s["e"], 1)

                    def turned(i):
                        for j in range(i + 1):
                            at = it * BLOCKS + i * (i + 1) // 2 + j
                            act.wait_ge(s["tp"], at + 1)
                            act.activation(eT[:, (i * (i + 1) // 2 + j) % 2, :], ps[:, 4 + (i * (i + 1) // 2 + j) % 2, :], ACT.Copy).then_inc(s["eT"], 1)
                        act.wait_ge(s["o"], it * TB + i + 1)
                        if i >= 2:
                            act.wait_ge(s["wo"], it * TB + i - 1)
                        act.activation(ao[:, i % 2, :, :].rearrange("p a b -> p (a b)"), ps[:, 6, :], ACT.Copy).then_inc(s["ao"], 1)

                    for i in range(TB):
                        for h in range(REP):
                            exps(i, h)
                        if i >= 1:
                            turned(i - 1)
                    turned(TB - 1)

        @block.tensor
        def _(pe):
            pe.wait_ge(s["cst"], 1)
            with pe.Fori(0, B) as b:
                pe.wait_ge(s["xn"], b + 1)
                pe.wait_ge(s["hs"], 1 + b * KV * TB)
                for q in range(4):
                    for j in range(4):
                        tr = pe.transpose(ps[:, q, j * P:(j + 1) * P],
                                          xn[:, 4 * (q % 2) + j, (q // 2) * P:(q // 2 + 1) * P], ident[:, :])
                    tr.then_inc(s["tr"], 1)
                with pe.Fori(0, KV) as kv:
                    it = b * KV + kv
                    pe.wait_ge(s["hT"], b * 4 + 4)
                    pe.wait_ge(s["w"], (it + 1) * 48)
                    pe.wait_ge(s["hs"], 1 + it * TB)
                    for i in range(NPROJ):
                        if i >= 2:
                            pe.wait_ge(s["rot"], it * NPROJ + i - 1)
                        for t in range(2):
                            for k in range(KC):
                                mm = pe.matmul(ps[:, 2 * (i % 2) + t, :], wq_s[:, k, i * HD:(i + 1) * HD] if i < REP else wk_s[:, k, :],
                                               hT[:, k, t * 512:(t + 1) * 512], start=(k == 0), stop=(k == KC - 1))
                        mm.then_inc(s["unit"], 1)
                    pe.wait_ge(s["rot"], it * NPROJ + NPROJ - 1)
                    for j in range(TB):
                        for k in range(KC):
                            mm = pe.matmul(ps[:, 2 * (NPROJ % 2) + j // 4, (j % 4) * P:(j % 4 + 1) * P], hT[:, k, j * P:(j + 1) * P],
                                           wv_s[:, k, :], start=(k == 0), stop=(k == KC - 1))
                    mm.then_inc(s["unit"], 1)
                    pe.wait_ge(s["rope"], it * NPROJ + NPROJ)

                    def scores(i, h):
                        n = NPROJ + 1 + i * REP + h
                        if i == 0 and h == 0:
                            pass
                        elif i == 0 and h == 1:
                            pe.wait_ge(s["v"], 1 + it + 1)
                        else:
                            pe.wait_ge(s["e"], it * REP * TB + i * REP + h - 1)
                        w = (i + 1) * P
                        for t in range(-(-w // 512)):
                            c0, c1 = t * 512, min(w, t * 512 + 512)
                            last = c1 == w
                            mm = pe.matmul(ps[:, 2 * (n % 2) + t, 0:c1 - c0], qT[:, h, i * P:(i + 1) * P], kT[:, c0:c1],
                                           start=True, stop=not last)
                            if last:
                                mm = pe.matmul(ps[:, 2 * (n % 2) + t, c1 - c0 - P:c1 - c0], ident_b[:, :], mask[:, :],
                                               start=False, stop=True)
                        mm.then_inc(s["unit"], 1)

                    def turn(i, j):
                        k = i * (i + 1) // 2 + j
                        at = it * BLOCKS + k
                        if j == 0:
                            pe.wait_ge(s["en"], it * REP * TB + (i + 1) * REP)
                        if k >= 2:
                            pe.wait_ge(s["eT"], at - 1)
                        for h in range(REP):
                            tr = pe.transpose(ps[:, 4 + k % 2, h * P:(h + 1) * P], e[:, i % 2, h, j * P:(j + 1) * P], ident[:, :])
                        tr.then_inc(s["tp"], 1)

                    def value(i, j):
                        at = it * BLOCKS + i * (i + 1) // 2 + j
                        pe.wait_ge(s["eT"], at + 1)
                        if j == 0 and i >= 1:
                            pe.wait_ge(s["ao"], it * TB + i)
                        mm = pe.matmul(ps[:, 6, :], v[:, j, :], eT[:, (i * (i + 1) // 2 + j) % 2, :], start=(j == 0), stop=(j == i))
                        if j == i:
                            mm.then_inc(s["o"], 1)

                    def out(i):
                        pe.wait_ge(s["ao"], it * TB + i + 1)
                        if i >= 1:
                            pe.wait_ge(s["hs"], 1 + it * TB + i)
                        for h in range(REP):
                            mm = pe.matmul(ps[:, 7, 0:D], ao[:, i % 2, h, :], flat(wo_s[:, ds(kv * REP + h), :]),
                                           start=(h == 0), stop=(h == REP - 1))
                        mm.then_inc(s["wo"], 1)

                    def attend(i):
                        for j in range(i + 1):
                            turn(i, j)
                            if j >= 1:
                                value(i, j - 1)
                        value(i, i)

                    for i in range(TB):
                        for h in range(REP):
                            scores(i, h)
                        if i >= 1:
                            attend(i - 1)
                        if i >= 2:
                            out(i - 2)
                    attend(TB - 1)
                    out(TB - 2)
                    out(TB - 1)



class Shared:
    pass


def program(nc, d, out):
    g = Shared()
    ctx = ExitStack()
    with ctx:
        g.x = ctx.enter_context(nc.sbuf_tensor("x", [P, NT, D], F32))
        g.mod = ctx.enter_context(nc.sbuf_tensor("mod", [P, B, 6 * D], F32))
        g.ident = ctx.enter_context(nc.sbuf_tensor("ident", [P, P], F32))
        g.ps = ctx.enter_context(nc.psum_tensor("ps", [P, 8, 512], F32))
        g.sel_dram, g.d = d["sel"], d

        def first(sp, s):
            sp.dma_start(g.x[:, :, :], d["hidden"].rearrange("(j p) d -> p j d", p=P)).then_inc(s, 16)
            sp.dma_start(g.ident[:, :], d["ident"]).then_inc(s, 16)
            return 2

        modulation(nc, g, 0, d["c0"], d["wmod0"], first)
        mamba(nc, g, d["w_in"], d["conv_w"], d["conv_b"], d["xproj"], d["dtw"], d["dtb"], d["a_log"], d["dskip"], d["w_out"])
        moe(nc, g, 0, 688, d["router0"], d["g0"], d["u0"], d["d0"])
        modulation(nc, g, 1, d["c1"], d["wmod1"])
        attn1(nc, g, d["q1"], d["k1"], d["v1"], d["fcw"], d["fcb"])
        hsctx = ExitStack()
        with hsctx:
            hs = hsctx.enter_context(nc.sbuf_tensor("hs", [P, NT, D], F32))
            attn2(nc, g, hs, d["n1"], d["wq"], d["wk"], d["wv"], d["wo"])
            moe(nc, g, 1, 512, d["router1"], d["g1"], d["u1"], d["d1"], hs, d["n2"])
        s_out = ctx.enter_context(nc.semaphore("s_out"))
        with nc.Block() as block:
            @block.sync
            def _(sp):
                sp.dma_start(out.rearrange("(j p) d -> p j d", p=P), g.x[:, :, :]).then_inc(s_out, 16)
                sp.wait_ge(s_out, 16)


def kernel(**inputs):
    import concourse.bacc as _bacc
    from concourse.bass_utils import run_bass_kernel_spmd as _run

    a = {k: np.asarray(v) for k, v in inputs.items()}
    T = np.ascontiguousarray
    chunked = lambda v: T(v.reshape(CD, P).T)
    xp = a["L0_attn_x_proj_w"]
    host = {
        "hidden": T(a["L0_attn_hidden_states"].reshape(B * L, D)),
        "ident": np.eye(P, dtype=np.float32),
        "sel": np.tile(np.eye(32, dtype=np.float32), (3, 1)),
        "c0": T(a["L0_c"]), "wmod0": T(a["L0_wmod"]), "c1": T(a["L1_c"]), "wmod1": T(a["L1_wmod"]),
        "w_in": T(a["L0_attn_in_proj_w"].T), "conv_w": T(a["L0_attn_conv_w"]), "conv_b": chunked(a["L0_attn_conv_b"]),
        "xproj": T(np.concatenate([xp[DTR:], xp[:DTR]], 0).T), "dtw": T(a["L0_attn_dt_proj_w"].T),
        "dtb": chunked(a["L0_attn_dt_proj_b"]), "a_log": T(a["L0_attn_A_log"]), "dskip": chunked(a["L0_attn_D"]),
        "w_out": T(a["L0_attn_out_proj_w"].T),
    }
    k = np.arange
    row16 = (k(NT) * P).astype(np.float32)
    row16[0] = 3e38
    wide = lambda v: T(np.broadcast_to(v.reshape(1, -1).astype(np.float32), (P, v.size)))
    freq = np.float32(1.0) / np.power(np.float32(1e6), k(0, HD, 2, dtype=np.float32) / np.float32(HD))
    ang = (k(L, dtype=np.float32)[:, None] * freq[None, :]).T
    host.update({
        "cos": np.concatenate([np.cos(ang), np.cos(ang)], 0).astype(np.float32),
        "sin": np.concatenate([np.sin(ang), -np.sin(ang)], 0).astype(np.float32),
        "mask": np.where(k(P)[None, :] > k(P)[:, None], np.float32(-3e38), np.float32(0)).astype(np.float32),
        "tri": (k(P)[:, None] < k(P)[None, :]).astype(np.float32), "ones": np.ones((P, P), np.float32),
        "e8": wide(k(EXP)), "row16": wide(row16), "row40": wide(k(SLOT_TILES)),
        "low8": wide((k(EXP)[None, :] < k(EXP)[:, None]).astype(np.float32)),
        "router0": T(a["L0_ffn_router_w"].T), "g0": T(a["L0_ffn_gate_w"].transpose(0, 2, 1)),
        "u0": T(a["L0_ffn_up_w"].transpose(0, 2, 1)), "d0": T(a["L0_ffn_down_w"].transpose(0, 2, 1)),
        "router1": T(a["L1_ffn_gate_w"]), "g1": T(a["L1_ffn_w1"]), "u1": T(a["L1_ffn_w3"]), "d1": T(a["L1_ffn_w2"]),
        "n1": T(a["L1_ffn_norm1_w"]), "n2": T(a["L1_ffn_norm2_w"]),
        "wq": T(a["L1_ffn_wq"]), "wk": T(a["L1_ffn_wk"]), "wv": T(a["L1_ffn_wv"]), "wo": T(a["L1_ffn_wo"]),
        "q1": T(a["L1_attn_Wq"].transpose(2, 0, 1).reshape(D, AH * D)),
        "k1": T(a["L1_attn_Wk"].transpose(2, 0, 1).reshape(D, AH * D)),
        "v1": T(a["L1_attn_Wv"].transpose(2, 0, 1).reshape(D, AH * D)),
        "fcw": T(a["L1_attn_fc_w"].T), "fcb": T(a["L1_attn_fc_b"].reshape(1, D)),
    })
    nc = _bacc.Bacc("TRN2", target_bir_lowering=False, num_devices=1)
    d = {k: nc.dram_tensor(f"in_{k}", v.shape, mybir.dt.from_np(v.dtype), kind="ExternalInput").ap() for k, v in host.items()}
    out = nc.dram_tensor("out_x", (B * L, D), F32, kind="ExternalOutput").ap()
    program(nc, d, out)
    r = _run(nc, [{f"in_{k}": v for k, v in host.items()}], core_ids=[0])
    return r.results[0]["out_x"].reshape(B, L, D)
```

```python
from contextlib import ExitStack, contextmanager

import numpy as np

import concourse.bass as bass
from concourse import mybir

P = 128
F32 = mybir.dt.float32
BF16 = mybir.dt.bfloat16
F32R = mybir.dt.float32r
I32 = mybir.dt.int32
U32 = mybir.dt.uint32
ALU = mybir.AluOpType
ACT = mybir.ActivationFunctionType
AX_X = mybir.AxisListType.X

B, L, D = 2, 1024, 256
NT = B * L // P
TB = L // P
KC = D // P
EPS = 1e-5
DI, NS, DTR, DC = 512, 16, 16, 4
CD = DI // P
EXP = 8
SLOT_TILES = 2 * NT + EXP - 1
AH = 3
H, KV, HD = 16, 4, 128
REP = H // KV
SA, CA, GA, SB, CB, GB = range(6)


class Own:

    def __init__(self, eng, sem):
        self.eng, self.sem, self.base, self.n = eng, sem, 0, 0

    def mark(self, ins):
        ins.then_inc(self.sem, 1)
        self.n += 1

    def wait(self):
        self.eng.wait_ge(self.sem, self.base + self.n)

    def __call__(self, ins):
        self.mark(ins)
        self.wait()

    @contextmanager
    def turn(self, i, count, per):
        base, n = self.base, self.n
        self.base, self.n = base + n + i * per, 0
        yield
        assert self.n == per, self.n
        self.base, self.n = base, n + count * per


def ds(i, n=1):
    return bass.ds(i, n)


def after(eng, sem, n):
    if not isinstance(n, int) or n > 0:
        eng.wait_ge(sem, n)


def flat(ap):
    return ap.rearrange("p a b -> p (a b)")



def dve_rstd(dve, own, src, nrm, g, turn, rms):
    st, mean, var, sd, rstd, t = nrm
    for j in range(NT):
        own.mark(dve.bn_stats(st[:, j, :], src[:, j, :]))
    own.wait()
    own(dve.tensor_tensor(mean[:, :], st[:, :, 1], st[:, :, 4], ALU.add))
    own(dve.tensor_tensor(t[:, :], st[:, :, 1], st[:, :, 4], ALU.subtract))
    own(dve.scalar_tensor_tensor(t[:, :], t[:, :], 0.25, t[:, :], ALU.mult, ALU.mult))
    own(dve.tensor_tensor(var[:, :], st[:, :, 2], st[:, :, 5], ALU.add))
    own(dve.scalar_tensor_tensor(var[:, :], var[:, :], 1.0 / D, t[:, :], ALU.mult, ALU.add))
    own(dve.tensor_scalar(mean[:, :], mean[:, :], 0.5, None, ALU.mult))
    if rms:
        own(dve.tensor_tensor(t[:, :], mean[:, :], mean[:, :], ALU.mult))
        own(dve.tensor_tensor(var[:, :], var[:, :], t[:, :], ALU.add))
    dve.tensor_scalar(var[:, :], var[:, :], EPS, None, ALU.add).then_inc(g.s_var, 1)
    dve.wait_ge(g.s_sd, g.norms + turn)
    own(dve.reciprocal(rstd[:, :], sd[:, :]))
    own(dve.tensor_tensor(t[:, :], var[:, :], rstd[:, :], ALU.mult))
    own(dve.tensor_tensor(t[:, :], t[:, :], rstd[:, :], ALU.mult))
    own(dve.tensor_scalar(t[:, :], t[:, :], -0.5, 1.5, ALU.mult, ALU.add))
    own(dve.tensor_tensor(rstd[:, :], rstd[:, :], t[:, :], ALU.mult))


def act_sqrt(act, nrm, g, turn):
    st, mean, var, sd, rstd, t = nrm
    act.wait_ge(g.s_var, g.norms + turn)
    act.activation(sd[:, :], var[:, :], ACT.Sqrt).then_inc(g.s_sd, 1)


def norm_buffers(sb, tag):
    return (sb(f"{tag}_st", [P, NT, 6]), sb(f"{tag}_mean", [P, NT]), sb(f"{tag}_var", [P, NT]),
            sb(f"{tag}_sd", [P, NT]), sb(f"{tag}_rstd", [P, NT]), sb(f"{tag}_t", [P, NT]))


def over(ap, n):
    p, d = ap.shape
    return ap.rearrange("p (a d) -> p a d", a=1).to_broadcast([p, n, d])


def modvec(mod, b, which):
    return mod[:, ds(b), ds(which * D, D)].rearrange("p a d -> p (a d)")



def modulation(nc, g, layer, c_in, wmod, first=None):
    ctx = ExitStack()
    with ctx:
        sb = lambda n, s, d=F32: ctx.enter_context(nc.sbuf_tensor(f"m{layer}_{n}", s, d))
        sem = lambda n: ctx.enter_context(nc.semaphore(f"m{layer}_{n}"))
        cT, sc, w = sb("cT", [P, KC, B]), sb("sc", [P, KC, B]), sb("w", [P, KC, 6 * D])
        sign, size = sb("sign", [P, B, 2, D]), sb("size", [P, B, 2, D])
        s_in, s_silu, s_mm, s_raw = g.mod_sems
        s_own = sem("own")
        LOADED = 16 * (B * KC + 1)
        mod, ps = g.mod, g.ps
        block = ctx.enter_context(nc.Block())

        @block.sync
        def _(sp):
            with nc.allow_non_contiguous_dma(reason="256 values"):
                for b in range(B):
                    for k in range(KC):
                        sp.dma_start(cT[:, k, b:b + 1], c_in[b, k * P:(k + 1) * P].rearrange("(p a) -> p a", a=1)).then_inc(s_in, 16)
            sp.dma_start(w[:, :, :], wmod.rearrange("(k p) n -> p k n", p=P)).then_inc(s_in, 16)
            if first is not None:
                n = first(sp, g.s_io)
                sp.wait_ge(g.s_io, 16 * n)

        @block.scalar
        def _(act):
            act.wait_ge(s_in, (layer + 1) * LOADED)
            act.activation(sc[:, :, :], cT[:, :, :], ACT.Silu).then_inc(s_silu, 1)
            act_sqrt(act, g.nrm, g, 1)
            for b in range(B):
                act.wait_ge(s_mm, layer * B + b + 1)
                act.activation(mod[:, b, :], ps[:, 4 * b:4 * b + 3, :].rearrange("p a n -> p (a n)"),
                               ACT.Copy).then_inc(s_raw, 1)

        @block.tensor
        def _(pe):
            pe.wait_ge(s_silu, layer + 1)
            for b in range(B):
                for n in range(3):
                    for k in range(KC):
                        mm = pe.matmul(ps[:, 4 * b + n, :], sc[:, k, b:b + 1].to_broadcast([P, P]),
                                       w[:, k, n * 512:(n + 1) * 512], start=(k == 0), stop=(k == KC - 1))
                mm.then_inc(s_mm, 1)

        @block.vector
        def _(dve):
            own = Own(dve, s_own)
            if first is not None:
                dve.wait_ge(g.s_io, 16 * 2)
            dve_rstd(dve, own, g.x, g.nrm, g, 1, False)
            dve.wait_ge(s_raw, (layer + 1) * B)
            v = mod[:, :, :].rearrange("p b (s d) -> p b s d", s=6)
            own.mark(dve.tensor_scalar(v[:, :, 1:6:3, :], v[:, :, 1:6:3, :], 1.0, None, ALU.add))
            own.mark(dve.tensor_scalar(sign[:, :, :, :], v[:, :, 2:6:3, :], 0.0, 2.0, ALU.is_ge, ALU.mult))
            for b in range(B):
                own(dve.scalar_tensor_tensor(size[:, b, :, :], v[:, b, 2:6:3, :], -1.0, v[:, b, 2:6:3, :],
                                             ALU.mult, ALU.max))
            own(dve.tensor_scalar(size[:, :, :, :], size[:, :, :, :], 0.25, None, ALU.max))
            for b in range(B):
                own(dve.scalar_tensor_tensor(v[:, b, 2:6:3, :], sign[:, b, :, :], 1.0, size[:, b, :, :],
                                             ALU.subtract, ALU.mult))
    g.norms += 1


def mamba(nc, g, w_in, conv_w, conv_b, xproj, dtw, dtb, a_log, dskip, w_out):
    ctx = ExitStack()
    with ctx:
        sb = lambda n, s, d=F32: ctx.enter_context(nc.sbuf_tensor(f"mb_{n}", s, d))
        sem = lambda n: ctx.enter_context(nc.semaphore(f"mb_{n}"))
        x, mod, ps, ident = g.x, g.mod, g.ps, g.ident
        win = sb("win", [P, KC, 2 * DI])
        wx = sb("wx", [P, CD, 2 * NS + DTR])
        wdt = sb("wdt", [DTR, DI])
        wout = sb("wout", [P, CD, D])
        cw, cb, db, dsk = sb("cw", [P, CD, DC]), sb("cb", [P, CD]), sb("db", [P, CD]), sb("dsk", [P, CD])
        am = sb("am", [P, CD, NS])
        sel, sel_f = sb("sel", [96, 32], BF16), sb("sel_f", [96, 32])
        nrm = g.nrm
        xp = sb("xp", [P, CD, L + DC - 1])
        z, xa, u = sb("z", [P, CD, L]), sb("xa", [P, CD, L]), sb("u", [P, CD, L])
        bb = sb("bb", [P, NS, L])
        xn = bb[:, 0:2, :].rearrange("p a (t d) -> p (a t) d", d=D)
        hT = bb[:, 2:4, :]
        xc = bb[:, 4:8, :]
        relu_v = bb[:, 4:8, :]
        abs_v = bb[:, 8:12, :]
        rest = bb[0:32, 15, :]
        xdt = sb("xdt", [DTR, L])
        mid = sb("mid", [32, L], BF16)
        parts = sb("parts", [96, L], BF16)
        dbx, h = sb("dbx", [P, 2, L]), sb("h", [P, 2, L])

        s_in = sem("in")
        s_own = sem("own")
        s_sel = sem("sel")
        s_pad = sem("pad")
        s_am = sem("am")
        s_xn = sem("xn")
        s_tr, s_hT = sem("tr"), sem("hT")
        s_ip = sem("ip")
        s_xp, s_z = sem("xp"), sem("z")
        s_tap, s_conv, s_xa = sem("tap"), sem("conv"), sem("xa")
        s_xd, s_parts = sem("xd"), sem("parts")
        s_dt = sem("dt")
        s_abs, s_exp, s_log, s_u = sem("abs"), sem("exp"), sem("log"), sem("u")
        s_bps = sem("bps")
        s_bb = [sem("bb_even"), sem("bb_odd")]
        HALF = NS // 2
        s_c, s_da, s_dbx = sem("c"), sem("da"), sem("dbx")
        s_g, s_y, s_gated = sem("g"), sem("y"), sem("gated")
        s_op, s_res = sem("op"), sem("res")
        block = ctx.enter_context(nc.Block())

        def pair(i):
            return flat(ps[:, 2 * i:2 * i + 2, :])

        @block.sync
        def _(sp):
            loads = [(win[:, :, :], w_in.rearrange("(k p) n -> p k n", p=P)),
                     (wx[:, :, :], xproj.rearrange("(k p) n -> p k n", p=P)),
                     (wdt[:, :], dtw), (wout[:, :, :], w_out.rearrange("(k p) n -> p k n", p=P)),
                     (cw[:, :, :], conv_w.rearrange("(k p) n -> p k n", p=P)),
                     (cb[:, :], conv_b), (db[:, :], dtb), (dsk[:, :], dskip),
                     (am[:, :, :], a_log.rearrange("(k p) n -> p k n", p=P)), (sel_f[:, :], g.sel_dram)]
            for dst, src in loads:
                sp.dma_start(dst, src).then_inc(s_in, 16)
            sp.wait_ge(s_in, 16 * len(loads))

        LOADED = 160

        @block.vector
        def _(dve):
            own = Own(dve, s_own)
            for primed in (s_g, s_gated, s_res):
                dve.sem_inc(primed, 1)
            dve.memset(xp[:, :, 0:DC - 1], 0.0).then_inc(s_pad, 1)
            with dve.Fori(0, B) as b, own.turn(b, B, TB + 1 + CD * 2 + 4 + CD + CD * (NS + 1) + TB):
                st, mean, var, sd, rstd, t = nrm
                for j in range(TB):
                    c = b * TB + j
                    own.mark(dve.tensor_scalar(xn[:, j, :], flat(x[:, ds(c), :]), mean[:, ds(c)], rstd[:, ds(c)],
                                               ALU.subtract, ALU.mult))
                own.wait()
                own(dve.tensor_tensor(xn, xn, over(modvec(mod, b, CA), TB), ALU.mult))
                dve.tensor_tensor(xn, xn, over(modvec(mod, b, SA), TB), ALU.add).then_inc(s_xn, 1)
                for k in range(CD):
                    dve.wait_ge(s_tap, b * CD + k + 1)
                    for tap in range(DC - 1):
                        ins = dve.scalar_tensor_tensor(xc[:, k, :], xp[:, k, tap:tap + L], cw[:, k, tap:tap + 1],
                                                       xc[:, k, :], ALU.mult, ALU.add)
                        if tap < DC - 2:
                            own(ins)
                        else:
                            ins.then_inc(s_conv, 1)
                dve.wait_ge(s_xd, b + 1)
                bc = flat(ps[0:32, 0:2, :])
                own.mark(dve.tensor_copy(xdt[:, :], flat(ps[32:48, 0:2, :])))
                own(dve.tensor_copy(parts[0:32, :], bc))
                own(dve.tensor_tensor(rest, bc, parts[0:32, :], ALU.subtract))
                own(dve.tensor_copy(mid[:, :], rest))
                dve.tensor_copy(parts[32:64, :], mid[:, :])
                dve.tensor_tensor(parts[64:96, :], rest, mid[:, :], ALU.subtract).then_inc(s_parts, 1)
                for k in range(CD):
                    dve.wait_ge(s_log, b * CD + k + 1)
                    own(dve.tensor_tensor(xp[:, k, DC - 1:], relu_v[:, k, :], abs_v[:, k, :], ALU.add))
                    dve.tensor_tensor(u[:, k, :], xp[:, k, DC - 1:], xa[:, k, :], ALU.mult).then_inc(s_u, 1)
                for n in range(1, NS, 2):
                    dve.wait_ge(s_bps, b * NS + n + 1)
                    dve.tensor_copy(bb[:, n, :], pair(n % 4)).then_inc(s_bb[1], 1)
                with dve.Fori(0, CD) as k, own.turn(k, CD, NS + 1):
                    for n in range(NS):
                        at = (b * CD + k) * NS + n
                        dve.wait_ge(s_da, at + 1)
                        dve.wait_ge(s_dbx, at + 1)
                        if n >= 2:
                            dve.wait_ge(s_y, at - 1)
                        own.mark(dve.tensor_tensor_scan(h[:, n % 2, :], pair(2 + n % 2), dbx[:, n % 2, :], 0.0,
                                                        ALU.mult, ALU.add))
                        own.wait()
                        for t in range(2):
                            dve.wait_ge(s_c, 2 * at + t + 1)
                            ht = h[:, n % 2, t * 512:(t + 1) * 512]
                            dve.tensor_tensor(ht, ht, ps[:, t, :], ALU.mult).then_inc(s_g, 1)
                    dve.wait_ge(s_y, (b * CD + k) * NS + NS)
                    dve.wait_ge(s_z, b * 8 + 8)
                    xk = flat(xa[:, ds(k), :])
                    own(dve.scalar_tensor_tensor(xk, xk, dsk[:, ds(k)], pair(1), ALU.mult, ALU.add))
                    dve.tensor_tensor(xk, xk, flat(z[:, ds(k), :]), ALU.mult).then_inc(s_gated, 1)
                for j in range(TB):
                    dve.wait_ge(s_op, b * TB + j + 1)
                    if j:
                        dve.wait_ge(s_res, 1 + b * TB + j)
                    xj = flat(x[:, ds(b * TB + j), :])
                    own(dve.tensor_tensor(h[:, 0, 0:D], ps[:, j, 0:D], modvec(mod, b, GA), ALU.mult))
                    dve.tensor_tensor(xj, xj, h[:, 0, 0:D], ALU.add).then_inc(s_res, 1)
                dve.wait_ge(s_res, 1 + b * TB + TB)

        @block.scalar
        def _(act):
            act.wait_ge(s_in, LOADED)
            act.activation(sel[:, :], sel_f[:, :], ACT.Copy).then_inc(s_sel, 1)
            act.activation(am[:, :, :], am[:, :, :], ACT.Exp).then_inc(s_am, 1)
            act.wait_ge(s_am, 1)
            act.activation(am[:, :, :], am[:, :, :], ACT.Copy, scale=-1.0).then_inc(s_am, 1)
            act.wait_ge(s_am, 2)
            act.wait_ge(s_pad, 1)
            with act.Fori(0, B) as b:
                for q in range(4):
                    act.wait_ge(s_tr, b * 4 + q + 1)
                    act.activation(hT[:, q // 2, (q % 2) * 512:(q % 2) * 512 + 512], ps[:, q, :], ACT.Copy).then_inc(s_hT, 1)
                for e in range(16):
                    act.wait_ge(s_ip, b * 16 + e + 1)
                    c, t = e // 2, e % 2
                    if c < CD:
                        act.activation(xp[:, c, DC - 1 + t * 512:DC - 1 + (t + 1) * 512], ps[:, e % 8, :],
                                       ACT.Copy).then_inc(s_xp, 1)
                    else:
                        act.activation(z[:, c - CD, t * 512:(t + 1) * 512], ps[:, e % 8, :], ACT.Silu).then_inc(s_z, 1)
                    if c < CD and t:
                        act.wait_ge(s_xp, b * 8 + e + 1)
                        act.activation(xc[:, c, :], xp[:, c, DC - 1:], ACT.Identity, bias=cb[:, c:c + 1],
                                       scale=cw[:, c, DC - 1:DC]).then_inc(s_tap, 1)
                for k in range(CD):
                    act.wait_ge(s_conv, b * CD + k + 1)
                    act.activation(xa[:, k, :], xc[:, k, :], ACT.Silu).then_inc(s_xa, 1)
                for k in range(CD):
                    act.wait_ge(s_dt, b * CD + k + 1)
                    act.activation(relu_v[:, k, :], pair(1 + k % 2), ACT.Relu, bias=db[:, k:k + 1])
                    act.activation(abs_v[:, k, :], pair(1 + k % 2), ACT.Abs, bias=db[:, k:k + 1]).then_inc(s_abs, 1)
                for k in range(CD):
                    act.wait_ge(s_abs, b * CD + k + 1)
                    act.activation(abs_v[:, k, :], abs_v[:, k, :], ACT.Exp, scale=-1.0).then_inc(s_exp, 1)
                for k in range(CD):
                    act.wait_ge(s_exp, b * CD + k + 1)
                    act.activation(abs_v[:, k, :], abs_v[:, k, :], ACT.Ln, bias=1.0).then_inc(s_log, 1)
                act.wait_ge(s_u, b * CD + CD)
                for n in range(0, NS, 2):
                    act.wait_ge(s_bps, b * NS + n + 1)
                    act.activation(bb[:, n, :], pair(n % 4), ACT.Copy).then_inc(s_bb[0], 1)
                for half in s_bb:
                    act.wait_ge(half, (b + 1) * HALF)
                with act.Fori(0, CD) as k:
                    act.wait_ge(s_gated, 1 + b * CD + k)
                    for n in range(NS):
                        at = (b * CD + k) * NS + n
                        if n >= 2:
                            act.wait_ge(s_g, 1 + 2 * (at - 1))
                        act.activation(pair(2 + n % 2), flat(xp[:, ds(k), DC - 1:]), ACT.Exp,
                                       scale=flat(am[:, ds(k), n:n + 1])).then_inc(s_da, 1)

        @block.gpsimd
        def _(pool):
            with pool.Fori(0, B) as b:
                for k in range(CD):
                    pool.wait_ge(s_gated, 1 + b * CD + k)
                    for n in range(NS):
                        at = (b * CD + k) * NS + n
                        pool.wait_ge(s_bb[n % 2], b * HALF + n // 2 + 1)
                        if n >= 2:
                            pool.wait_ge(s_g, 1 + 2 * (at - 1))
                        pool.tensor_tensor(dbx[:, n % 2, :], u[:, k, :], bb[:, n, :], ALU.mult).then_inc(s_dbx, 1)

        @block.tensor
        def _(pe):
            pe.wait_ge(s_in, LOADED)
            pe.wait_ge(s_sel, 1)
            with pe.Fori(0, B) as b:
                pe.wait_ge(s_xn, b + 1)
                pe.wait_ge(s_res, 1 + b * TB)
                for q in range(4):
                    for j in range(4):
                        tr = pe.transpose(ps[:, q, j * P:(j + 1) * P],
                                          xn[:, 4 * (q % 2) + j, (q // 2) * P:(q // 2 + 1) * P], ident[:, :])
                    tr.then_inc(s_tr, 1)
                pe.wait_ge(s_hT, b * 4 + 4)
                for e in range(16):
                    if e >= 8:
                        pe.wait_ge(s_xp, b * 8 + e - 7)
                    c, t = e // 2, e % 2
                    for k in range(KC):
                        mm = pe.matmul(ps[:, e % 8, :], win[:, k, c * P:(c + 1) * P], hT[:, k, t * 512:(t + 1) * 512],
                                       start=(k == 0), stop=(k == KC - 1))
                    mm.then_inc(s_ip, 1)
                pe.wait_ge(s_z, b * 8 + 8)
                for k in range(CD):
                    pe.wait_ge(s_xa, b * CD + k + 1)
                    for t in range(2):
                        mm = pe.matmul(ps[0:48, t, :], wx[:, k, :], xa[:, k, t * 512:(t + 1) * 512],
                                       start=(k == 0), stop=(k == CD - 1))
                mm.then_inc(s_xd, 1)
                pe.wait_ge(s_parts, b + 1)
                for k in range(CD):
                    if k >= 2:
                        pe.wait_ge(s_abs, b * CD + k - 1)
                    for t in range(2):
                        mm = pe.matmul(ps[:, 2 + 2 * (k % 2) + t, :], wdt[:, k * P:(k + 1) * P],
                                       xdt[:, t * 512:(t + 1) * 512], start=True, stop=True)
                    mm.then_inc(s_dt, 1)
                pe.wait_ge(s_abs, b * CD + CD)
                for n in range(NS):
                    if n >= 4:
                        pe.wait_ge(s_bb[n % 2], b * HALF + n // 2 - 1)
                    for t in range(2):
                        mm = pe.matmul(ps[:, 2 * (n % 4) + t, :], sel[:, n:n + 1].to_broadcast([96, P]),
                                       parts[:, t * 512:(t + 1) * 512], start=True, stop=True)
                    mm.then_inc(s_bps, 1)
                with pe.Fori(0, CD) as k:
                    for half in s_bb:
                        pe.wait_ge(half, (b + 1) * HALF)

                    def c_row(n, t, at):
                        pe.wait_ge(s_g, 1 + 2 * at + (t + 1 if n else 0))
                        pe.matmul(ps[:, t, :], sel[:, NS + n:NS + n + 1].to_broadcast([96, P]),
                                  parts[:, t * 512:(t + 1) * 512], start=True, stop=True).then_inc(s_c, 1)

                    for t in range(2):
                        c_row(0, t, (b * CD + k) * NS)
                    pe.wait_ge(s_gated, 1 + b * CD + k)
                    for n in range(NS):
                        at = (b * CD + k) * NS + n
                        for t in range(2):
                            if n + 1 < NS:
                                c_row(n + 1, t, at)
                            else:
                                pe.wait_ge(s_g, 1 + 2 * at + t + 1)
                            mm = pe.matmul(ps[:, 2 + t, :], ident[:, :], h[:, n % 2, t * 512:(t + 1) * 512],
                                           start=(n == 0), stop=(n == NS - 1))
                        mm.then_inc(s_y, 1)
                pe.wait_ge(s_gated, 1 + b * CD + CD)
                for j in range(TB):
                    for k in range(CD):
                        mm = pe.matmul(ps[:, j, 0:D], xa[:, k, j * P:(j + 1) * P], wout[:, k, :],
                                       start=(k == 0), stop=(k == CD - 1))
                    mm.then_inc(s_op, 1)


def moe(nc, g, layer, F, router, gate_w, up_w, down_w, hs=None, norm_w=None):
    ctx = ExitStack()
    with ctx:
        sb = lambda n, s, d=F32: ctx.enter_context(nc.sbuf_tensor(f"e{layer}_{n}", s, d))
        sem = lambda n: ctx.enter_context(nc.semaphore(f"e{layer}_{n}"))
        x, mod, ps, ident = g.x, g.mod, g.ps, g.ident
        FB = 1 if F <= 512 else 2
        FN = F // FB
        FCH = [(c * P, min(P, F - c * P)) for c in range(-(-F // P))]
        NF = len(FCH)
        FULL = F // P
        S = SLOT_TILES
        assert S % 2 == 1
        wg, wu = sb("wg", [P, EXP, KC, F]), sb("wu", [P, EXP, KC, F])
        wd = sb("wd", [P, EXP, NF, D])
        xn = sb("xn", [P, NT, D])
        nrm = norm_buffers(sb, f"e{layer}_n")
        tri, ones = sb("tri", [P, P]), sb("ones", [P, P])
        rw = sb("rw", [P, KC, EXP])
        xT = sb("xT", [P, 2, 4 * P])
        hT = sb("hT", [P, 2, NF * P])
        xin = sb("xin", [P, 2, D])
        sg, hh = sb("sg", [P, F]), sb("hh", [P, F])
        yo = sb("yo", [P, 2, D])
        zero = yo[:, 0, :]
        nwb = sb("nwb", [P, D]) if norm_w is not None else None
        cut = lambda t, a, n, m: t[:, a:a + n * m].rearrange("p (a b) -> p a b", a=n)
        lg, top = cut(sg, 0, NT, EXP), cut(sg, 128, NT, 8)
        idx = sb("idx", [P, NT, 8], U32)
        idf = sb("idf", [P, 2, NT])
        hot = sb("hot", [P, 2, NT, EXP])
        m, rank, tot, incl = (sb(n, [P, NT, EXP]) for n in ("m", "rank", "tot", "incl"))
        e8, row16 = sb("e8", [P, EXP]), sb("row16", [P, NT])
        row40 = sb("row40", [P, S])
        low8 = sb("low8", [P, EXP, EXP])
        one16 = sb("one16", [P, NT])
        cmp, tmp8, cmp_tile = cut(sg, 256, EXP, NT), cut(sg, 384, EXP, EXP), cut(hh, 0, S, EXP)
        cnt, first8 = sb("cnt", [P, EXP]), sb("first8", [P, EXP])
        texp_f, texp = sb("texp_f", [P, S]), sb("texp", [P, S], I32)
        posf, pos = sb("posf", [P, 2, NT]), sb("pos", [P, 2, NT], U32)
        prob, ex, den = sb("prob", [P, 2, NT]), sb("ex", [P, NT]), sb("den", [P, NT])
        GR = 4
        gat = wg[:, 0, :, :].rearrange("p a b -> p (a b)")[:, 0:D * 4].rearrange("p (r d) -> p r d", d=D)
        gat2 = wg[:, 1, :, :].rearrange("p a b -> p (a b)")[:, 0:D * 4].rearrange("p (r d) -> p r d", d=D)
        slots = nc.dram_tensor(f"e{layer}_slots", [S * P, D], F32, kind="Internal").ap()
        outs = nc.dram_tensor(f"e{layer}_outs", [S * P, D], F32, kind="Internal").ap()

        s_in, s_w, s_z, s_zm = sem("in"), sem("w"), sem("z"), sem("zm")
        s_own, s_xn = sem("own"), sem("xn")
        s_tr, s_xT, s_lg = sem("tr"), sem("xT"), sem("lg")
        s_ex, s_exd, s_m, s_rank = g.moe_sems
        s_texp, s_pos, s_sc = sem("texp"), sem("pos"), sem("sc")
        s_xin = [sem("xin0"), sem("xin1")]
        s_xtp, s_xts, s_gu, s_sg, s_h = sem("xtp"), sem("xts"), sem("gu"), sem("sg"), sem("h")
        s_thp, s_hts, s_y, s_ys = sem("thp"), sem("hts"), sem("y"), sem("ys")
        s_st = [sem("st0"), sem("st1")]
        s_ga = [sem(f"ga{r}") for r in range(GR)]
        s_comb, s_res = sem("comb"), sem("res")
        block = ctx.enter_context(nc.Block())
        NCONST = 7 + (norm_w is not None)

        @block.sync
        def _(sp):
            consts = [(tri[:, :], g.d["tri"]), (ones[:, :], g.d["ones"]), (e8[:, :], g.d["e8"]), (row16[:, :], g.d["row16"]),
                      (row40[:, :], g.d["row40"]), (low8[:, :, :], g.d["low8"].rearrange("p (a b) -> p a b", a=EXP)),
                      (rw[:, :, :], router.rearrange("(k p) e -> p k e", p=P))]
            if norm_w is not None:
                consts.append((nwb[:, :], norm_w.rearrange("(a n) -> a n", a=1).to_broadcast([P, D])))
            for dst, src in consts:
                sp.dma_start(dst, src).then_inc(s_in, 16)
            sp.wait_ge(s_zm, 1)
            sp.dma_start(slots.rearrange("(t p) d -> p t d", p=P), over(zero, S)).then_inc(s_z, 16)
            for e in range(EXP):
                sp.dma_start(wg[:, e, :, :], gate_w[e].rearrange("(k p) f -> p k f", p=P)).then_inc(s_w, 16)
                sp.dma_start(wu[:, e, :, :], up_w[e].rearrange("(k p) f -> p k f", p=P)).then_inc(s_w, 16)
                sp.dma_start(wd[:, e, 0:FULL, :], down_w[e, 0:FULL * P].rearrange("(c p) d -> p c d", p=P)).then_inc(s_w, 16)
                if FULL < NF:
                    sp.dma_start(wd[0:F - FULL * P, e, FULL, :], down_w[e, FULL * P:F]).then_inc(s_w, 16)
            sp.wait_ge(s_sc, 16 * 2 * NT)

            def load_pair(i2, tiles=2):
                for q in range(tiles):
                    i = i2 * 2 + q
                    after(sp, s_xtp, i2 * 2)
                    sp.dma_start(xin[:, q, :], slots[ds(i * P, P), :]).then_inc(s_xin[q], 16)

            load_pair(0)
            with sp.Fori(1, S // 2) as i2:
                load_pair(i2)
            load_pair(S // 2, 1)

        WLOADS = EXP * (3 + (FULL < NF)) * 16

        @block.gpsimd
        def _(pool):
            pool.wait_ge(s_z, 16)
            pool.wait_ge(s_pos, 1)
            for j in range(NT):
                for k in range(2):
                    pool.indirect_dma_start(slots[:, :], bass.IndirectOffsetOnAxis(ap=pos[:, k, j:j + 1], axis=0),
                                            xn[:, j, :], None).then_inc(s_sc, 16)

            def store(i2, q):
                pool.wait_ge(s_ys, i2 * 2 + q + 1)
                pool.dma_start(outs[ds((i2 * 2 + q) * P, P), :], yo[:, q, :]).then_inc(s_st[q], 16)

            with pool.Fori(0, S // 2) as i2:
                store(i2, 0)
                store(i2, 1)
            store(S // 2, 0)
            for q in range(2):
                pool.wait_ge(s_st[q], 16 * ((S + 1 - q) // 2))
            for j in range(NT):
                r = j % GR
                if j >= GR:
                    pool.wait_ge(s_comb, j - GR + 1)
                for k, dst in enumerate((gat, gat2)):
                    pool.indirect_dma_start(dst[:, r, :], None, outs[:, :],
                                            bass.IndirectOffsetOnAxis(ap=pos[:, k, j:j + 1], axis=0)).then_inc(s_ga[r], 16)

        @block.scalar
        def _(act):
            act_sqrt(act, nrm, g, 1)
            for r in range(NT // 2):
                act.wait_ge(s_tr, r + 1)
                if r >= 2:
                    act.wait_ge(s_lg, 2 * (r - 1))
                act.activation(xT[:, r % 2, :], ps[:, r % 2, :], ACT.Copy).then_inc(s_xT, 1)
            act.wait_ge(s_exd, layer + 1)
            act.activation(ex[:, :], ex[:, :], ACT.Exp).then_inc(s_ex, 1)

            def tile_pair(i2, tiles=2):
                for q in range(tiles):
                    i = i2 * 2 + q
                    act.wait_ge(s_gu, i + 1)
                    after(act, s_h, i)
                    act.activation(sg[:, :].rearrange("p (a n) -> p a n", a=FB), ps[:, 0:FB, 0:FN], ACT.Silu).then_inc(s_sg, 1)
                    act.wait_ge(s_thp, i + 1)
                    half = NF // 2
                    for a in range(2):
                        n = half if a == 0 else NF - half
                        act_i = act.activation(hT[:, q, a * half * P:(a * half + n) * P], ps[:, 4 + a, 0:n * P], ACT.Copy)
                    act_i.then_inc(s_hts, 1)

            tile_pair(0)
            with act.Fori(1, S // 2) as i2:
                tile_pair(i2)
            tile_pair(S // 2, 1)

        @block.tensor
        def _(pe):
            pe.wait_ge(s_xn, 1)
            pe.wait_ge(s_in, 16 * NCONST)
            def logits(r):
                for t in range(2):
                    j = 2 * r + t
                    for k in range(KC):
                        mm = pe.matmul(ps[:, 7, j * EXP:(j + 1) * EXP], xT[:, r % 2, (2 * t + k) * P:(2 * t + k + 1) * P],
                                       rw[:, k, :], start=(k == 0), stop=(k == KC - 1))
                    mm.then_inc(s_lg, 1)
            for r in range(NT // 2):
                if r >= 2:
                    pe.wait_ge(s_xT, r - 1)
                for t in range(2):
                    for k in range(KC):
                        tr = pe.transpose(ps[:, r % 2, (2 * t + k) * P:(2 * t + k + 1) * P],
                                          xn[:, 2 * r + t, k * P:(k + 1) * P], ident[:, :])
                tr.then_inc(s_tr, 1)
                if r >= 1:
                    pe.wait_ge(s_xT, r)
                    logits(r - 1)
            pe.wait_ge(s_xT, NT // 2)
            logits(NT // 2 - 1)
            pe.wait_ge(s_m, layer + 1)
            pe.matmul(ps[:, 2, 0:P], tri[:, :], m[:, :, :].rearrange("p a b -> p (a b)"), start=True, stop=True)
            pe.matmul(ps[:, 3, 0:P], ones[:, :], m[:, :, :].rearrange("p a b -> p (a b)"), start=True, stop=True).then_inc(s_rank, 1)
            pe.wait_ge(s_texp, 1)
            pe.wait_ge(s_w, WLOADS)

            def turn_x(i, q, loads):
                pe.wait_ge(s_xin[q], 16 * loads)
                after(pe, s_xts, i)
                for k in range(KC):
                    tr = pe.transpose(ps[:, 7, k * P:(k + 1) * P], xin[:, q, k * P:(k + 1) * P], ident[:, :])
                tr.then_inc(s_xtp, 1)

            def gate_up(i, q):
                e = pe.value_load(texp[0:1, ds(i)], min_val=0, max_val=EXP - 1)
                pe.wait_ge(s_xts, i + 1)
                after(pe, s_h, i)
                for w, b0 in ((wg, 0), (wu, 2)):
                    for k in range(KC):
                        for a in range(FB):
                            mm = pe.matmul(ps[:, b0 + a, 0:FN], xT[:, q, k * P:(k + 1) * P],
                                           w[:, ds(e), k, a * FN:(a + 1) * FN].rearrange("p a n -> p (a n)"),
                                           start=(k == 0), stop=(k == KC - 1))
                mm.then_inc(s_gu, 1)

            def turn_h(i):
                pe.wait_ge(s_h, i + 1)
                after(pe, s_hts, i)
                half = NF // 2
                for c, (f0, n) in enumerate(FCH):
                    a, col = (0, c) if c < half else (1, c - half)
                    tr = pe.transpose(ps[0:n, 4 + a, col * P:(col + 1) * P], hh[:, f0:f0 + n], ident[:, :])
                tr.then_inc(s_thp, 1)

            def down(i, q, yfree):
                e = pe.value_load(texp[0:1, ds(i)], min_val=0, max_val=EXP - 1)
                pe.wait_ge(s_hts, i + 1)
                after(pe, s_ys, yfree)
                for c, (f0, n) in enumerate(FCH):
                    mm = pe.matmul(ps[:, 6, 0:D], hT[0:n, q, c * P:(c + 1) * P],
                                   wd[0:n, ds(e), c, :].rearrange("p a n -> p (a n)"), start=(c == 0), stop=(c == NF - 1))
                mm.then_inc(s_y, 1)

            turn_x(0, 0, 1)
            gate_up(0, 0)
            turn_x(1, 1, 1)
            turn_h(0)

            def tile_pair(i2, last=False):
                for q in (1, 0):
                    i = i2 * 2 + (1 if q else 2)
                    gate_up(i, q)
                    down(i - 1, 1 - q, i - 1)
                    if not (last and q == 0):
                        turn_x(i + 1, 1 - q, i2 + 2)
                    turn_h(i)

            tile_pair(0)
            with pe.Fori(1, S // 2 - 1) as i2:
                tile_pair(i2)
            tile_pair(S // 2 - 1, True)
            down(S - 1, 0, S - 1)

        @block.vector
        def _(dve):
            own = Own(dve, s_own)
            dve.memset(zero, 0.0).then_inc(s_zm, 1)
            own(dve.memset(one16[:, :], 1.0))
            st, mean, var, sd, rstd, t = nrm
            if hs is None:
                dve_rstd(dve, own, x, nrm, g, 1, False)
                for j in range(NT):
                    own.mark(dve.tensor_scalar(xn[:, j, :], x[:, j, :], mean[:, j:j + 1], rstd[:, j:j + 1],
                                               ALU.subtract, ALU.mult))
                own.wait()
                for b in range(B):
                    v = xn[:, b * TB:(b + 1) * TB, :]
                    own(dve.tensor_tensor(v, v, over(mod[:, b, CB * D:(CB + 1) * D], TB), ALU.mult))
                    ins = dve.tensor_tensor(v, v, over(mod[:, b, SB * D:(SB + 1) * D], TB), ALU.add)
                ins.then_inc(s_xn, 1)
            else:
                dve_rstd(dve, own, hs, nrm, g, 1, True)
                dve.wait_ge(s_in, 16 * NCONST)
                own.wait()
                for j in range(NT):
                    ins = dve.scalar_tensor_tensor(xn[:, j, :], hs[:, j, :], rstd[:, j:j + 1], nwb[:, :], ALU.mult, ALU.mult)
                ins.then_inc(s_xn, 1)
            dve.wait_ge(s_in, 16 * NCONST)
            dve.wait_ge(s_lg, NT)
            own(dve.tensor_copy(lg, ps[:, 7, 0:P].rearrange("p (a b) -> p a b", a=NT)))
            for j in range(NT):
                own.mark(dve.max(top[:, j, :], lg[:, j, :]))
            own.wait()
            for j in range(NT):
                own.mark(dve.max_index(idx[:, j, :], top[:, j, :], lg[:, j, :]))
            dve.tensor_tensor(ex[:, :], top[:, :, 1], top[:, :, 0], ALU.subtract).then_inc(s_exd, 1)
            own.wait()
            own(dve.tensor_copy(idf[:, :, :], idx[:, :, 0:2].rearrange("p j k -> p k j")))
            for k in range(2):
                own.mark(dve.tensor_tensor(hot[:, k, :, :], over(e8[:, :], NT),
                                           idf[:, k, :].rearrange("p (j a) -> p j a", a=1).to_broadcast([P, NT, EXP]), ALU.is_equal))
            own.wait()
            dve.tensor_tensor(m[:, :, :], hot[:, 0, :, :], hot[:, 1, :, :], ALU.add).then_inc(s_m, 1)
            dve.wait_ge(s_ex, layer + 1)
            own(dve.tensor_scalar(den[:, :], ex[:, :], 1.0, None, ALU.add))
            own(dve.reciprocal(prob[:, 0, :], den[:, :]))
            own(dve.tensor_tensor(prob[:, 1, :], prob[:, 0, :], ex[:, :], ALU.mult))
            dve.wait_ge(s_rank, layer + 1)
            own.mark(dve.tensor_copy(rank[:, :, :], ps[:, 2, 0:P].rearrange("p (a b) -> p a b", a=NT)))
            own(dve.tensor_copy(tot[:, :, :], ps[:, 3, 0:P].rearrange("p (a b) -> p a b", a=NT)))
            for e in range(EXP):
                own.mark(dve.tensor_tensor_scan(incl[:, :, e], one16[:, :], tot[:, :, e], 0.0, ALU.mult, ALU.add))
            own.wait()
            own(dve.tensor_tensor(tot[:, :, :], incl[:, :, :], tot[:, :, :], ALU.subtract))
            own(dve.tensor_tensor(rank[:, :, :], rank[:, :, :], tot[:, :, :], ALU.add))
            own(dve.tensor_tensor(cmp, incl[:, NT - 1, :].rearrange("p (e a) -> p e a", a=1).to_broadcast([P, EXP, NT]),
                                  over(row16[:, :], EXP), ALU.is_gt))
            own(dve.tensor_reduce(cnt[:, :], cmp, AX_X, ALU.add))
            own(dve.tensor_scalar(cnt[:, :], cnt[:, :], 1.0, None, ALU.add))
            own(dve.tensor_tensor(tmp8, low8[:, :, :], over(cnt[:, :], EXP), ALU.mult))
            own(dve.tensor_reduce(first8[:, :], tmp8, AX_X, ALU.add))
            own(dve.tensor_tensor(cmp_tile, row40[:, :].rearrange("p (s a) -> p s a", a=1).to_broadcast([P, S, EXP]),
                                  over(first8[:, :], S), ALU.is_ge))
            own(dve.tensor_reduce(texp_f[:, :], cmp_tile, AX_X, ALU.add))
            own(dve.tensor_scalar(texp_f[:, :], texp_f[:, :], -1.0, None, ALU.add))
            dve.tensor_copy(texp[:, :], texp_f[:, :]).then_inc(s_texp, 1)
            own(dve.tensor_scalar(first8[:, :], first8[:, :], float(P), None, ALU.mult))
            own(dve.tensor_tensor(rank[:, :, :], rank[:, :, :], over(first8[:, :], NT), ALU.add))
            for k in range(2):
                own.mark(dve.tensor_tensor(hot[:, k, :, :], hot[:, k, :, :], rank[:, :, :], ALU.mult))
            own.wait()
            for k in range(2):
                own.mark(dve.tensor_reduce(posf[:, k, :], hot[:, k, :, :], AX_X, ALU.add))
            own.wait()
            dve.tensor_copy(pos[:, :, :], posf[:, :, :]).then_inc(s_pos, 1)

            def take_x(i, q):
                dve.wait_ge(s_xtp, i + 1)
                dve.tensor_copy(xT[:, q, 0:D], ps[:, 7, 0:D]).then_inc(s_xts, 1)

            def take_y(i, q, stores):
                dve.wait_ge(s_y, i + 1)
                after(dve, s_st[q], 16 * stores)
                dve.tensor_copy(yo[:, q, :], ps[:, 6, 0:D]).then_inc(s_ys, 1)

            def hidden(i):
                dve.wait_ge(s_sg, i + 1)
                after(dve, s_thp, i)
                dve.tensor_tensor(hh[:, :].rearrange("p (a n) -> p a n", a=FB), sg[:, :].rearrange("p (a n) -> p a n", a=FB),
                                  ps[:, 2:2 + FB, 0:FN], ALU.mult).then_inc(s_h, 1)

            take_x(0, 0)
            hidden(0)
            take_x(1, 1)

            def tile_pair(i2, last=False):
                for q in (1, 0):
                    i = i2 * 2 + (1 if q else 2)
                    hidden(i)
                    take_y(i - 1, 1 - q, i2)
                    if not (last and q == 0):
                        take_x(i + 1, 1 - q)

            tile_pair(0)
            with dve.Fori(1, S // 2 - 1) as i2:
                tile_pair(i2)
            tile_pair(S // 2 - 1, True)
            take_y(S - 1, 0, S // 2)
            for j in range(NT):
                r = j % GR
                dve.wait_ge(s_ga[r], 32 * (j // GR + 1))
                own(dve.tensor_scalar(gat[:, r, :], gat[:, r, :], prob[:, 0, j:j + 1], None, ALU.mult))
                own(dve.scalar_tensor_tensor(gat2[:, r, :], gat2[:, r, :], prob[:, 1, j:j + 1], gat[:, r, :], ALU.mult, ALU.add))
                if hs is not None:
                    own(dve.tensor_tensor(gat2[:, r, :], gat2[:, r, :], hs[:, j, :], ALU.add))
                own(dve.tensor_tensor(gat2[:, r, :], gat2[:, r, :], mod[:, j // TB, GB * D:(GB + 1) * D], ALU.mult))
                dve.tensor_tensor(x[:, j, :], x[:, j, :], gat2[:, r, :], ALU.add).then_inc(s_comb, 1)
    g.norms += 1


def attn1(nc, g, wq, wk, wv, fc_w, fc_b):
    ctx = ExitStack()
    with ctx:
        sb = lambda n, s, d=F32: ctx.enter_context(nc.sbuf_tensor(f"a1_{n}", s, d))
        sem = lambda n: ctx.enter_context(nc.semaphore(f"a1_{n}"))
        x, mod, ps, ident = g.x, g.mod, g.ps, g.ident
        SCALE = 1.0 / float(np.sqrt(np.float32(D)))
        w = {n: sb("w" + n, [P, KC, AH * D]) for n in "qkv"}
        fw, fb, ones = sb("fw", [P, KC, D]), sb("fb", [1, D]), sb("ones", [1, P])
        nrm = g.nrm
        HI, LO = 0, 1
        THREE = ((HI, HI), (HI, LO), (LO, HI))
        hT = [sb("hT" + half, [P, KC, L], F32R) for half in ("hi", "lo")]
        wh = [sb("w" + half, [P, 3, KC, D], F32R) for half in ("hi", "lo")]
        qT, kT = ([sb(n + half, [P, 2, KC, L], F32R) for half in ("hi", "lo")] for n in ("qT", "kT"))
        v = sb("v", [P, 2, TB, D])
        e = sb("e", [P, 2, L])
        xn = flat(e[:, :, :]).rearrange("p (a b) -> p a b", a=TB)
        aT = e
        LAG = 2
        RING = LAG + 1
        eh = [sb("e" + half, [P, RING, L], F32R) for half in ("hi", "lo")]
        vs = sb("vs", [P, 2, D])
        vh = [sb("v" + half, [P, RING, D], F32R) for half in ("hi", "lo")]
        mx, nb, sm, rc = (sb(n, [P, TB]) for n in ("mx", "nb", "sm", "rc"))
        t1 = sb("t1", [P, 2, D])
        s_in, s_own, s_xn = sem("in"), sem("own"), sem("xn")
        s_tr, s_hT, s_hl = sem("tr"), sem("hT"), sem("hl")
        s_wh, s_wl = sem("wh"), sem("wl")
        s_unit, s_free = sem("unit"), sem("free")
        s_lo = sem("lo")
        s_eh, s_el = sem("eh"), sem("el")
        s_nb, s_vs, s_av = sem("nb"), sem("vs"), sem("av")
        s_aT, s_res = sem("aT"), sem("res")
        block = ctx.enter_context(nc.Block())
        PROJ = 6
        PER_HEAD = PROJ + TB
        UNITS = AH * PER_HEAD

        def pair(i):
            return flat(ps[:, 2 * i:2 * i + 2, :])

        def order():
            todo = [("proj", 0, i) for i in range(PROJ)]
            for h in range(AH):
                for m in range(TB):
                    todo.append(("score", h, m))
                    if m == TB // 2 and h + 1 < AH:
                        todo += [("proj", h + 1, i) for i in range(PROJ)]
            return todo

        todo = order()
        assert len(todo) == UNITS and UNITS % 2 == 0
        read_at = {h: 1 + max(n for n, (kind, hh, _) in enumerate(todo) if kind == "proj" and hh == h) for h in range(AH)}

        @block.sync
        def _(sp):
            for n, src in (("q", wq), ("k", wk), ("v", wv)):
                sp.dma_start(w[n][:, :, :], src.rearrange("(k p) n -> p k n", p=P)).then_inc(s_in, 16)
            sp.dma_start(fw[:, :, :], fc_w.rearrange("(k p) n -> p k n", p=P)).then_inc(s_in, 16)
            sp.dma_start(fb[:, :], fc_b).then_inc(s_in, 16)
            sp.dma_start(ones[:, :], g.d["ones"][0:1, :]).then_inc(s_in, 16)
            sp.wait_ge(s_in, 96)

        @block.tensor
        def _(pe):
            pe.sem_inc(s_av, 1)
            pe.wait_ge(s_in, 96)

            def project(b, n, h, i):
                unit_free(b, n)
                o = n % 2
                if i == 0:
                    pe.wait_ge(s_wl, b * AH + h + 1)
                if i < 4:
                    for t in range(2):
                        for k in range(KC):
                            for x_, y_ in THREE:
                                mm = pe.matmul(ps[:, 2 * o + t, :], wh[x_][:, i // 2, k, (i % 2) * P:(i % 2 + 1) * P],
                                               hT[y_][:, k, t * 512:(t + 1) * 512], start=(k == 0 and x_ == y_),
                                               stop=(k == KC - 1 and x_ == LO))
                else:
                    for t in range(4):
                        j = (i - 4) * 4 + t
                        for k in range(KC):
                            for x_, y_ in THREE:
                                mm = pe.matmul(ps[:, 2 * o + t // 2, (t % 2) * D:(t % 2 + 1) * D], hT[x_][:, k, j * P:(j + 1) * P],
                                               wh[y_][:, 2, k, :], start=(k == 0 and x_ == y_), stop=(k == KC - 1 and x_ == LO))
                mm.then_inc(s_unit, 1)

            def unit_free(b, n):
                if n >= 2:
                    pe.wait_ge(s_free, b * UNITS + n - 1)
                    kind, h, i = todo[n - 2]
                    if kind == "proj" and i < 4:
                        pe.wait_ge(s_lo, (b * AH + h) * 4 + i + 1)

            def scores(b, n, h, m):
                unit_free(b, n)
                if m == 0:
                    pe.wait_ge(s_free, b * UNITS + read_at[h])
                    pe.wait_ge(s_lo, (b * AH + h) * 4 + 4)
                for t in range(2):
                    for k in range(KC):
                        for x_, y_ in THREE:
                            mm = pe.matmul(ps[:, 2 * (n % 2) + t, :], kT[x_][:, h % 2, k, m * P:(m + 1) * P],
                                           qT[y_][:, h % 2, k, t * 512:(t + 1) * 512], start=(k == 0 and x_ == y_),
                                           stop=(k == KC - 1 and x_ == LO))
                mm.then_inc(s_unit, 1)

            def values(b, h, m):
                at = (b * AH + h) * TB + m
                q = (h * TB + m) % RING
                pe.wait_ge(s_vs, at + 1)
                pe.wait_ge(s_el, at + 1)
                for c in range(KC):
                    for t in range(2):
                        for x_, y_ in THREE:
                            mm = pe.matmul(ps[:, 4 + 2 * c + t, :], vh[x_][:, q, c * P:(c + 1) * P], eh[y_][:, q, t * 512:(t + 1) * 512],
                                           start=(h == 0 and m == 0 and x_ == y_), stop=(h == AH - 1 and m == TB - 1 and x_ == LO))
                mm.then_inc(s_av, 1)

            with pe.Fori(0, B) as b:
                pe.wait_ge(s_xn, b + 1)
                pe.wait_ge(s_aT, 1 + 2 * b)
                for q in range(4):
                    for j in range(4):
                        tr = pe.transpose(ps[:, 4 + q, j * P:(j + 1) * P],
                                          xn[:, 4 * (q % 2) + j, (q // 2) * P:(q // 2 + 1) * P], ident[:, :])
                    tr.then_inc(s_tr, 1)
                pe.wait_ge(s_hl, b * 4 + 4)
                pe.wait_ge(s_res, 1 + b * TB)
                late = []
                for n, (kind, h, i) in enumerate(todo):
                    if kind == "proj":
                        project(b, n, h, i)
                    else:
                        scores(b, n, h, i)
                        late.append((h, i))
                        if len(late) > LAG:
                            values(b, *late.pop(0))
                for h, i in late:
                    values(b, h, i)
                pe.wait_ge(s_aT, 1 + 2 * b + 2)
                pe.wait_ge(s_free, b * UNITS + UNITS)
                for j in range(TB):
                    o = ps[:, j // 2, (j % 2) * D:(j % 2 + 1) * D]
                    for k in range(KC):
                        pe.matmul(o, aT[:, k, j * P:(j + 1) * P], fw[:, k, :], start=(k == 0), stop=False)
                    mm = pe.matmul(o, ones[:, :], fb[:, :], start=False, stop=True)
                mm.then_inc(s_unit, 1)

        @block.scalar
        def _(act):
            act.sem_inc(s_aT, 1)
            act.wait_ge(s_in, 96)
            with act.Fori(0, B) as b:
                def high_weights(h):
                    for i, n in enumerate("qkv"):
                        ins = act.activation(wh[HI][:, i, :, :], w[n][:, :, h * D:(h + 1) * D], ACT.Copy)
                    ins.then_inc(s_wh, 1)

                high_weights(0)
                for q in range(4):
                    act.wait_ge(s_tr, b * 4 + q + 1)
                    act.activation(hT[HI][:, q // 2, (q % 2) * 512:(q % 2) * 512 + 512], ps[:, 4 + q, :], ACT.Copy).then_inc(s_hT, 1)
                for n, (kind, h, i) in enumerate(todo):
                    act.wait_ge(s_unit, b * (UNITS + 1) + n + 1)
                    if kind == "proj":
                        if h >= 2 and i == 0:
                            act.wait_ge(s_av, 1 + (b * AH + h - 1) * TB)
                        if h < 2 and i == 0:
                            act.wait_ge(s_av, 1 + b * AH * TB)
                        dst = (qT[HI][:, h % 2, i, :] if i < 2 else kT[HI][:, h % 2, i - 2, :] if i < 4 else
                               flat(v[:, h % 2, (i - 4) * 4:(i - 4) * 4 + 4, :]))
                        act.activation(dst, pair(n % 2), ACT.Copy).then_inc(s_free, 1)
                    else:
                        at = (b * AH + h) * TB + i
                        act.wait_ge(s_nb, at + 1)
                        if i >= 2 or h >= 1:
                            act.wait_ge(s_el, at - 1)
                        act.activation(e[:, i % 2, :], pair(n % 2), ACT.Exp, bias=nb[:, i:i + 1], scale=SCALE,
                                       accum_out=sm[:, i:i + 1]).then_inc(s_free, 1)
                        act.wait_ge(s_free, b * UNITS + n + 1)
                        if i >= RING or h >= 1:
                            act.wait_ge(s_av, 1 + at - RING + 1)
                        act.activation(eh[HI][:, (h * TB + i) % RING, :], e[:, i % 2, :], ACT.Copy).then_inc(s_eh, 1)
                        if i == 1 and h + 1 < AH:
                            high_weights(h + 1)
                for k in range(KC):
                    act.wait_ge(s_av, 1 + (b + 1) * AH * TB)
                    act.activation(aT[:, k, :], pair(2 + k), ACT.Copy).then_inc(s_aT, 1)

        @block.vector
        def _(dve):
            own = Own(dve, s_own)
            dve.sem_inc(s_res, 1)
            st, mean, var, sd, rstd, t = nrm
            with dve.Fori(0, B) as b, own.turn(b, B, TB + 1 + AH * TB * 4 + TB):
                for j in range(TB):
                    c = b * TB + j
                    own.mark(dve.tensor_scalar(xn[:, j, :], flat(x[:, ds(c), :]), mean[:, ds(c)], rstd[:, ds(c)],
                                               ALU.subtract, ALU.mult))
                own.wait()
                own(dve.tensor_tensor(xn[:, :, :], xn[:, :, :], over(modvec(mod, b, CA), TB), ALU.mult))
                dve.tensor_tensor(xn[:, :, :], xn[:, :, :], over(modvec(mod, b, SA), TB), ALU.add).then_inc(s_xn, 1)
                for q in range(4):
                    dve.wait_ge(s_hT, b * 4 + q + 1)
                    at = (slice(None), q // 2, slice((q % 2) * 512, (q % 2) * 512 + 512))
                    dve.tensor_tensor(hT[LO][at], ps[:, 4 + q, :], hT[HI][at].bitcast(F32), ALU.subtract).then_inc(s_hl, 1)
                late = None

                def value_rows(n, h, m):
                    at = (b * AH + h) * TB + m
                    dve.wait_ge(s_free, b * UNITS + n + 1)
                    own(dve.reciprocal(rc[:, m:m + 1], sm[:, m:m + 1]))
                    q = (h * TB + m) % RING
                    own(dve.tensor_scalar(vs[:, m % 2, :], v[:, h % 2, m, :], rc[:, m:m + 1], 1.0 / AH, ALU.mult, ALU.mult))
                    if h > 0 or m >= RING:
                        dve.wait_ge(s_av, 1 + at - RING + 1)
                    own(dve.tensor_copy(vh[HI][:, q, :], vs[:, m % 2, :]))
                    dve.tensor_tensor(vh[LO][:, q, :], vs[:, m % 2, :], vh[HI][:, q, :].bitcast(F32), ALU.subtract).then_inc(s_vs, 1)

                for n, (kind, h, i) in enumerate(todo):
                    if kind == "proj" and i < 4:
                        hi, lo = ((qT, kT)[i // 2][half][:, h % 2, i % 2, :] for half in (HI, LO))
                        dve.wait_ge(s_free, b * UNITS + n + 1)
                        dve.tensor_tensor(lo, pair(n % 2), hi.bitcast(F32), ALU.subtract).then_inc(s_lo, 1)
                    elif kind == "score":
                        if late is not None:
                            value_rows(*late)
                        late = (n, h, i)
                        dve.wait_ge(s_unit, b * (UNITS + 1) + n + 1)
                        own(dve.reduce_max(mx[:, i:i + 1], pair(n % 2), AX_X))
                        dve.tensor_scalar(nb[:, i:i + 1], mx[:, i:i + 1], -SCALE, None, ALU.mult).then_inc(s_nb, 1)
                value_rows(*late)
                for j in range(TB):
                    dve.wait_ge(s_unit, (b + 1) * (UNITS + 1))
                    if j >= 2:
                        dve.wait_ge(s_res, 1 + b * TB + j - 1)
                    xj = flat(x[:, ds(b * TB + j), :])
                    own(dve.tensor_tensor(t1[:, j % 2, :], ps[:, j // 2, (j % 2) * D:(j % 2 + 1) * D], modvec(mod, b, GA), ALU.mult))
                    dve.tensor_tensor(xj, xj, t1[:, j % 2, :], ALU.add).then_inc(s_res, 1)
                dve.wait_ge(s_res, 1 + b * TB + TB)



        @block.gpsimd
        def _(pool):
            with pool.Fori(0, B) as b:
                def low_weights(h):
                    pool.wait_ge(s_wh, b * AH + h + 1)
                    for i, n in enumerate("qkv"):
                        ins = pool.tensor_tensor(wh[LO][:, i, :, :], w[n][:, :, h * D:(h + 1) * D], wh[HI][:, i, :, :].bitcast(F32),
                                                 ALU.subtract)
                    ins.then_inc(s_wl, 1)

                low_weights(0)
                for h in range(AH):
                    for m in range(TB):
                        q, at = (h * TB + m) % RING, (b * AH + h) * TB + m
                        pool.wait_ge(s_eh, at + 1)
                        pool.tensor_tensor(eh[LO][:, q, :], e[:, m % 2, :], eh[HI][:, q, :].bitcast(F32), ALU.subtract).then_inc(s_el, 1)
                        if m == 1 and h + 1 < AH:
                            low_weights(h + 1)


def attn2(nc, g, hs, norm_w, wq, wk, wv, wo):
    ctx = ExitStack()
    with ctx:
        sb = lambda n, s, d=F32: ctx.enter_context(nc.sbuf_tensor(f"a2_{n}", s, d))
        sem = lambda n: ctx.enter_context(nc.semaphore(f"a2_{n}"))
        x, mod, ps, ident = g.x, g.mod, g.ps, g.ident
        SCALE = 1.0 / float(np.sqrt(HD))
        nrm = norm_buffers(sb, "a2_n")
        nwb = sb("nwb", [P, D])
        WC = (REP + 2) * HD
        w_s = sb("w", [P, KC, WC])
        WPIECE, WPIECES = 256, WC // 256
        wo_s = sb("wo", [P, H, D])
        cos, sin = sb("cos", [P, L]), sb("sin", [P, L])
        mask_f, mask, ident_b = sb("mask_f", [P, P]), sb("mask", [P, P], BF16), sb("ident_b", [P, P], BF16)
        HI, LO = 0, 1
        hT, wh, qT, kT, v, eT = ([
            sb(n + half, shape, F32R) for half in ("hi", "lo")] for n, shape in (
            ("hT", [P, KC, L]), ("wh", [P, KC, WC]), ("qT", [P, REP, L]), ("kT", [P, L]), ("v", [P, TB, HD]), ("eT", [P, 3, REP * P])))
        THREE = ((HI, HI), (HI, LO), (LO, HI))
        e = sb("e", [P, 2, REP, L])
        xn = e[:, 1, 0:2, :].rearrange("p a (b d) -> p (a b) d", d=D)
        r1, r2 = e[:, 0, 0:2, :], e[:, 0, 2:4, :]
        ao = sb("ao", [P, 2, REP, P])
        mx, nb, sm, rc = (sb(n, [P, 2 * REP]) for n in ("mx", "nb", "sm", "rc"))
        names = ("in", "own", "xn", "tr", "hT", "hlow", "whigh", "wlow", "cst", "unit", "w", "rot", "sum", "high", "rope", "rope_k",
                 "v", "vlow", "nb", "e", "rc", "en", "en_last",
                 "tp", "eT", "eTlow", "o", "ao", "wo", "hs")
        s = {n: sem(n) for n in names}
        block = ctx.enter_context(nc.Block())
        NPROJ = REP + 1
        UNITS = NPROJ + 1 + REP * TB
        BLOCKS = TB * (TB + 1) // 2

        def pair(i, w=L, p=slice(0, P)):
            return flat(ps[p, 2 * i:2 * i + 2, :])[:, 0:w]

        def sequence():
            early = {(TB - 2, TB - 2): [("project", 0, 0), ("project", 1, 0)], (TB - 1, TB - 1): [("split", NPROJ - 2, 0), ("project", NPROJ, 0)]}
            for i in range(2, NPROJ):
                early[TB - 1, 2 * i - 3] = [("split", i - 2, 0), ("project", i, 0)]
            todo, turned = [("score", 0, h) for h in range(REP)], []

            def take(i, j):
                todo.append(("turn", i, j))
                turned.append((i, j))
                if len(turned) > 2:
                    value(*turned.pop(0))

            def value(i, j):
                if j == min(i, 1) and i >= 1:
                    todo.append(("out", i - 1, 0))
                todo.append(("value", i, j))

            for i in range(TB):
                for j in range(i + 1):
                    if i + 1 < TB:
                        for h in range(REP):
                            if h * (i + 1) // (REP + 1) == j:
                                todo.append(("score", i + 1, h))
                    take(i, j)
                    todo.extend(early.get((i, j), []))
                if i in PIECE_AFTER:
                    todo.append(("weights", PIECE_AFTER.index(i), 0))
            while turned:
                value(*turned.pop(0))
            return todo + [("split", NPROJ - 1, 0), ("out", TB - 1, 0)]

        PIECE_AFTER = (2, 3, 4)
        assert len(PIECE_AFTER) == WPIECES
        steps = sequence()

        def key_heads(eng, b, body):
            with eng.Fori(0, KV - 1) as kv:
                body(kv, True)
            body(KV - 1, False)
        act_steps = list(steps)
        for n in range(len(steps) - 1):
            if act_steps[n][0] == "score" and act_steps[n + 1][0] == "turn" and act_steps[n + 1][2] > 0:
                act_steps[n], act_steps[n + 1] = act_steps[n + 1], act_steps[n]
        SMALL = 2
        ring = [x for x in steps if x[0] in ("turn", "out")]
        bank = {x: (4, 5, 7)[r % 3] for r, x in enumerate(ring)}

        @block.sync
        def _(sp):
            loads = [(nwb[:, :], norm_w.rearrange("(a n) -> a n", a=1).to_broadcast([P, D])),
                     (wo_s[:, :, :], wo.rearrange("(h p) d -> p h d", p=P)), (cos[:, :], g.d["cos"]), (sin[:, :], g.d["sin"]),
                     (mask_f[:, :], g.d["mask"])]
            for dst, src in loads:
                sp.dma_start(dst, src).then_inc(s["in"], 16)
            with sp.Fori(0, B) as b:
                with sp.Fori(0, KV) as kv:
                    it = b * KV + kv
                    sp.wait_ge(s["v"], 1 + it)
                    sp.dma_start(w_s[:, :, 0:REP * HD], wq.rearrange("(k p) n -> p k n", p=P)[:, :, ds(kv * (REP * HD), REP * HD)]).then_inc(s["w"], 16)
                    sp.dma_start(w_s[:, :, REP * HD:(REP + 1) * HD], wk.rearrange("(k p) n -> p k n", p=P)[:, :, ds(kv * HD, HD)]).then_inc(s["w"], 16)
                    sp.dma_start(w_s[:, :, (REP + 1) * HD:WC], wv.rearrange("(k p) n -> p k n", p=P)[:, :, ds(kv * HD, HD)]).then_inc(s["w"], 16)

        @block.vector
        def _(dve):
            own = Own(dve, s["own"])
            dve.sem_inc(s["hs"], 1)
            st, mean, var, sd, rstd, t = nrm
            dve_rstd(dve, own, x, nrm, g, 1, False)
            for j in range(NT):
                own.mark(dve.tensor_scalar(hs[:, j, :], x[:, j, :], mean[:, j:j + 1], rstd[:, j:j + 1], ALU.subtract, ALU.mult))
            own.wait()
            for b in range(B):
                h = hs[:, b * TB:(b + 1) * TB, :]
                own(dve.tensor_tensor(h, h, over(mod[:, b, CB * D:(CB + 1) * D], TB), ALU.mult))
                own(dve.tensor_tensor(h, h, over(mod[:, b, SB * D:(SB + 1) * D], TB), ALU.add))
            dve_rstd(dve, own, hs, nrm, g, 2, True)
            dve.wait_ge(s["in"], 80)
            dve.tensor_copy(mask[:, :], mask_f[:, :])
            dve.tensor_copy(ident_b[:, :], ident[:, :]).then_inc(s["cst"], 1)
            with dve.Fori(0, B) as b, own.turn(b, B, KV * (REP * TB + TB)):
                for j in range(TB):
                    c = b * TB + j
                    ins = dve.scalar_tensor_tensor(xn[:, j, :], flat(hs[:, ds(c), :]), rstd[:, ds(c)], nwb[:, :], ALU.mult, ALU.mult)
                ins.then_inc(s["xn"], 1)
                for q in range(4):
                    dve.wait_ge(s["hT"], b * 4 + q + 1)
                    at = (slice(None), q // 2, slice((q % 2) * 512, (q % 2) * 512 + 512))
                    dve.tensor_tensor(hT[LO][at], ps[:, q, :], hT[HI][at].bitcast(F32), ALU.subtract).then_inc(s["hlow"], 1)

                def rope(it, i):
                    dve.wait_ge(s["unit"], it * UNITS + i + 1)
                    if i >= 2:
                        dve.wait_ge(s["rope"], it * REP + i - 1)
                    dve.tensor_tensor(r1[:, i % 2, :], pair(i % 2), cos[:, :], ALU.mult)
                    dve.tensor_tensor(r2[0:64, i % 2, :], pair(i % 2, L, slice(64, P)), sin[64:P, :], ALU.mult)
                    dve.tensor_tensor(r2[64:P, i % 2, :], pair(i % 2, L, slice(0, 64)), sin[0:64, :],
                                      ALU.mult).then_inc(s["rot"], 1)

                def split_key(it):
                    dve.wait_ge(s["high"], it * NPROJ + NPROJ)
                    dve.tensor_tensor(kT[LO][:, :], r1[:, REP % 2, :], kT[HI][:, :].bitcast(F32), ALU.subtract).then_inc(s["rope_k"], 1)

                for i in range(NPROJ):
                    rope(b * KV, i)
                split_key(b * KV)

                def body(kv, follows):
                    it = b * KV + kv
                    dve.wait_ge(s["v"], 1 + it + 1)
                    dve.tensor_tensor(flat(v[LO][:, :, :]), pair(NPROJ % 2), flat(v[HI][:, :, :]).bitcast(F32),
                                      ALU.subtract).then_inc(s["vlow"], 1)
                    late, turned = None, []

                    def low(i, j):
                        k = i * (i + 1) // 2 + j
                        dve.wait_ge(s["eT"], it * BLOCKS + k + 1)
                        dve.tensor_tensor(eT[LO][:, k % 3, :], ps[:, bank["turn", i, j], :], eT[HI][:, k % 3, :].bitcast(F32),
                                          ALU.subtract).then_inc(s["eTlow"], 1)

                    def normal(i, h):
                        q, at = (i % 2) * REP + h, it * REP * TB + i * REP + h
                        dve.wait_ge(s["e"], at + 1)
                        if h < REP - 1:
                            dve.reciprocal(rc[:, q:q + 1], sm[:, q:q + 1]).then_inc(s["rc"], 1)
                        else:
                            own(dve.reciprocal(rc[:, q:q + 1], sm[:, q:q + 1]))
                            dve.tensor_scalar(e[:, i % 2, h, 0:(i + 1) * P], e[:, i % 2, h, 0:(i + 1) * P], rc[:, q:q + 1],
                                              None, ALU.mult).then_inc(s["en_last"], 1)

                    for what, i, h in steps:
                        if what == "score":
                            if i > SMALL:
                                normal(*late)
                            n, q = NPROJ + 1 + i * REP + h, (i % 2) * REP + h
                            dve.wait_ge(s["unit"], it * UNITS + n + 1)
                            own(dve.reduce_max(mx[:, q:q + 1], pair(n % 2, (i + 1) * P), AX_X))
                            dve.tensor_scalar(nb[:, q:q + 1], mx[:, q:q + 1], -SCALE, None, ALU.mult).then_inc(s["nb"], 1)
                            if i <= SMALL and late is not None:
                                normal(*late)
                            late = (i, h)
                        elif what == "turn":
                            if turned:
                                low(*turned.pop(0))
                            turned.append((i, h))
                            if (i, h) == (TB - 2, TB - 2):
                                normal(*late)
                        elif what == "value":
                            if (i, h) in turned:
                                low(*turned.pop(0))
                        elif what == "project" and follows:
                            if turned:
                                low(*turned.pop(0))
                            if i < NPROJ:
                                rope(it + 1, i)
                        elif (what, i) == ("split", NPROJ - 1) and follows:
                            split_key(it + 1)
                        elif what == "out":
                            hj = flat(hs[:, ds(b * TB + i), :])
                            dve.wait_ge(s["wo"], it * TB + i + 1)
                            dve.tensor_tensor(hj, ps[:, bank[what, i, h], 0:D], hj, ALU.add).then_inc(s["hs"], 1)

                with dve.Fori(0, KV - 1) as kv, own.turn(kv, KV - 1, REP * TB + TB):
                    body(kv, True)
                body(KV - 1, False)

        @block.gpsimd
        def _(pool):
            with pool.Fori(0, B) as b:
                def add(it, i):
                    pool.wait_ge(s["rot"], it * NPROJ + i + 1)
                    pool.tensor_tensor(r1[:, i % 2, :], r1[:, i % 2, :], r2[:, i % 2, :], ALU.add).then_inc(s["sum"], 1)
                    if i < REP:
                        pool.wait_ge(s["high"], it * NPROJ + i + 1)
                        pool.tensor_tensor(qT[LO][:, i, :], r1[:, i % 2, :], qT[HI][:, i, :].bitcast(F32), ALU.subtract).then_inc(s["rope"], 1)

                def low_weights(it, c):
                    at = (slice(None), slice(None), slice(c * WPIECE, (c + 1) * WPIECE))
                    pool.wait_ge(s["whigh"], it * WPIECES + c + 1)
                    pool.tensor_tensor(wh[LO][at], w_s[at], wh[HI][at].bitcast(F32), ALU.subtract).then_inc(s["wlow"], 1)

                for c in range(WPIECES):
                    low_weights(b * KV, c)
                for i in range(NPROJ):
                    add(b * KV, i)

                def body(kv, follows):
                    it = b * KV + kv
                    for i in range(TB):
                        for h in range(REP - 1):
                            q = (i % 2) * REP + h
                            pool.wait_ge(s["rc"], it * (REP - 1) * TB + i * (REP - 1) + h + 1)
                            pool.tensor_tensor(e[:, i % 2, h, 0:(i + 1) * P], e[:, i % 2, h, 0:(i + 1) * P],
                                               rc[:, q:q + 1].to_broadcast([P, (i + 1) * P]), ALU.mult).then_inc(s["en"], 1)
                        if follows and i - 1 in PIECE_AFTER:
                            low_weights(it + 1, PIECE_AFTER.index(i - 1))
                    for i in range(NPROJ if follows else 0):
                        add(it + 1, i)

                key_heads(pool, b, body)

        @block.scalar
        def _(act):
            act.sem_inc(s["v"], 1)
            act_sqrt(act, nrm, g, 1)
            act_sqrt(act, nrm, g, 2)
            with act.Fori(0, B) as b:
                def high_weights(it, c):
                    at = (slice(None), slice(None), slice(c * WPIECE, (c + 1) * WPIECE))
                    act.wait_ge(s["w"], (it + 1) * 48)
                    act.activation(wh[HI][at], w_s[at], ACT.Copy).then_inc(s["whigh"], 1)

                for c in range(WPIECES):
                    high_weights(b * KV, c)
                for q in range(4):
                    act.wait_ge(s["tr"], b * 4 + q + 1)
                    act.activation(hT[HI][:, q // 2, (q % 2) * 512:(q % 2) * 512 + 512], ps[:, q, :], ACT.Copy).then_inc(s["hT"], 1)

                def high(it, i):
                    act.wait_ge(s["sum"], it * NPROJ + i + 1)
                    act.activation(qT[HI][:, i, :] if i < REP else kT[HI][:, :], r1[:, i % 2, :], ACT.Copy).then_inc(s["high"], 1)

                for i in range(NPROJ):
                    high(b * KV, i)

                def body(kv, follows):
                    it = b * KV + kv
                    act.wait_ge(s["unit"], it * UNITS + NPROJ + 1)
                    act.activation(flat(v[HI][:, :, :]), pair(NPROJ % 2), ACT.Copy).then_inc(s["v"], 1)

                    def exponentials(i, h):
                        n = NPROJ + 1 + i * REP + h
                        q, at = (i % 2) * REP + h, it * REP * TB + i * REP + h
                        act.wait_ge(s["nb"], at + 1)
                        if h == 0 and i >= 2:
                            act.wait_ge(s["tp"], it * BLOCKS + i * (i - 1) // 2)
                        act.activation(e[:, i % 2, h, 0:(i + 1) * P], pair(n % 2, (i + 1) * P), ACT.Exp, bias=nb[:, q:q + 1],
                                       scale=SCALE, accum_out=sm[:, q:q + 1]).then_inc(s["e"], 1)

                    for what, i, h in act_steps:
                        if what == "score":
                            exponentials(i, h)
                        elif what == "split" and follows:
                            high(it + 1, i)
                        elif what == "weights" and follows:
                            high_weights(it + 1, i)
                        elif what == "turn":
                            k = i * (i + 1) // 2 + h
                            act.wait_ge(s["tp"], it * BLOCKS + k + 1)
                            act.activation(eT[HI][:, k % 3, :], ps[:, bank[what, i, h], :], ACT.Copy).then_inc(s["eT"], 1)
                        elif what == "value" and h == i:
                            act.wait_ge(s["o"], it * TB + i + 1)
                            if i >= 2:
                                act.wait_ge(s["wo"], it * TB + i - 1)
                            act.activation(ao[:, i % 2, :, :].rearrange("p a b -> p (a b)"), ps[:, 6, :], ACT.Copy).then_inc(s["ao"], 1)

                key_heads(act, b, body)

        @block.tensor
        def _(pe):
            pe.wait_ge(s["cst"], 1)
            with pe.Fori(0, B) as b:
                pe.wait_ge(s["xn"], b + 1)
                pe.wait_ge(s["hs"], 1 + b * KV * TB)
                for q in range(4):
                    for j in range(4):
                        tr = pe.transpose(ps[:, q, j * P:(j + 1) * P],
                                          xn[:, 4 * (q % 2) + j, (q // 2) * P:(q // 2 + 1) * P], ident[:, :])
                    tr.then_inc(s["tr"], 1)
                pe.wait_ge(s["hlow"], b * 4 + 4)

                def project(it, i):
                    if i == 0:
                        pe.wait_ge(s["wlow"], (it + 1) * WPIECES)
                    if i >= 2:
                        pe.wait_ge(s["rot"], it * NPROJ + i - 1)
                    for t in range(2):
                        for k in range(KC):
                            for x_, y_ in THREE:
                                mm = pe.matmul(ps[:, 2 * (i % 2) + t, :], wh[x_][:, k, i * HD:(i + 1) * HD],
                                               hT[y_][:, k, t * 512:(t + 1) * 512], start=(k == 0 and x_ == y_),
                                               stop=(k == KC - 1 and x_ == LO))
                    mm.then_inc(s["unit"], 1)

                def project_values(it):
                    pe.wait_ge(s["rot"], it * NPROJ + NPROJ - 1)
                    for j in range(TB):
                        for k in range(KC):
                            for x_, y_ in THREE:
                                mm = pe.matmul(ps[:, 2 * (NPROJ % 2) + j // 4, (j % 4) * P:(j % 4 + 1) * P],
                                               hT[x_][:, k, j * P:(j + 1) * P], wh[y_][:, k, NPROJ * HD:WC],
                                               start=(k == 0 and x_ == y_), stop=(k == KC - 1 and x_ == LO))
                    mm.then_inc(s["unit"], 1)

                for i in range(NPROJ):
                    project(b * KV, i)
                project_values(b * KV)

                def body(kv, follows):
                    it = b * KV + kv
                    pe.wait_ge(s["rope"], it * REP + REP)
                    pe.wait_ge(s["rope_k"], it + 1)

                    def scores(i, h):
                        n = NPROJ + 1 + i * REP + h
                        if i == 0 and h == 0:
                            pass
                        elif i == 0 and h == 1:
                            pe.wait_ge(s["vlow"], it + 1)
                        else:
                            pe.wait_ge(s["e"], it * REP * TB + i * REP + h - 1)
                        w = (i + 1) * P
                        for t in range(-(-w // 512)):
                            c0, c1 = t * 512, min(w, t * 512 + 512)
                            last = c1 == w
                            for x_, y_ in THREE:
                                mm = pe.matmul(ps[:, 2 * (n % 2) + t, 0:c1 - c0], qT[x_][:, h, i * P:(i + 1) * P], kT[y_][:, c0:c1],
                                               start=(x_ == y_), stop=(x_ == LO and not last))
                            if last:
                                mm = pe.matmul(ps[:, 2 * (n % 2) + t, c1 - c0 - P:c1 - c0], ident_b[:, :], mask[:, :],
                                               start=False, stop=True)
                        mm.then_inc(s["unit"], 1)

                    def ring_free(r):
                        if r == 0:
                            pe.wait_ge(s["hs"], 1 + it * TB)
                        if r >= 3:
                            what, i, j = ring[r - 3]
                            if what == "turn":
                                pe.wait_ge(s["eTlow"], it * BLOCKS + i * (i + 1) // 2 + j + 1)
                            else:
                                pe.wait_ge(s["hs"], 1 + it * TB + i + 1)

                    for what, i, j in steps:
                        if what == "score":
                            scores(i, j)
                        elif what in ("split", "weights"):
                            continue
                        elif what == "project":
                            if follows and i == NPROJ:
                                project_values(it + 1)
                            elif follows:
                                if i < 2:
                                    pe.wait_ge(s["e"], (it + 1) * REP * TB - 1 + i)
                                project(it + 1, i)
                        elif what == "turn":
                            if j == 0:
                                pe.wait_ge(s["en"], (it * TB + i + 1) * (REP - 1))
                                pe.wait_ge(s["en_last"], it * TB + i + 1)
                            ring_free(ring.index((what, i, j)))
                            for h in range(REP):
                                tr = pe.transpose(ps[:, bank[what, i, j], h * P:(h + 1) * P], e[:, i % 2, h, j * P:(j + 1) * P], ident[:, :])
                            tr.then_inc(s["tp"], 1)
                        elif what == "value":
                            k = i * (i + 1) // 2 + j
                            pe.wait_ge(s["eTlow"], it * BLOCKS + k + 1)
                            if j == 0 and i >= 1:
                                pe.wait_ge(s["ao"], it * TB + i)
                            for x_, y_ in THREE:
                                mm = pe.matmul(ps[:, 6, :], v[x_][:, j, :], eT[y_][:, k % 3, :], start=(j == 0 and x_ == y_),
                                               stop=(j == i and x_ == LO))
                            if j == i:
                                mm.then_inc(s["o"], 1)
                        else:
                            pe.wait_ge(s["ao"], it * TB + i + 1)
                            ring_free(ring.index((what, i, j)))
                            for h in range(REP):
                                mm = pe.matmul(ps[:, bank[what, i, j], 0:D], ao[:, i % 2, h, :], flat(wo_s[:, ds(kv * REP + h), :]),
                                               start=(h == 0), stop=(h == REP - 1))
                            mm.then_inc(s["wo"], 1)

                key_heads(pe, b, body)

    g.norms += 2


class Shared:
    pass


def program(nc, d, out):
    g = Shared()
    ctx = ExitStack()
    with ctx:
        g.x = ctx.enter_context(nc.sbuf_tensor("x", [P, NT, D], F32))
        g.mod = ctx.enter_context(nc.sbuf_tensor("mod", [P, B, 6 * D], F32))
        g.ident = ctx.enter_context(nc.sbuf_tensor("ident", [P, P], F32))
        g.ps = ctx.enter_context(nc.psum_tensor("ps", [P, 8, 512], F32))
        g.s_var, g.s_sd = (ctx.enter_context(nc.semaphore(n)) for n in ("var", "sd"))
        g.s_io = ctx.enter_context(nc.semaphore("io"))
        g.mod_sems = [ctx.enter_context(nc.semaphore(f"mod_{n}")) for n in ("in", "silu", "mm", "raw")]
        g.moe_sems = [ctx.enter_context(nc.semaphore(f"moe_{n}")) for n in ("ex", "exd", "m", "rank")]
        g.norms = 0
        g.nrm = norm_buffers(lambda n, s: ctx.enter_context(nc.sbuf_tensor(n, s, F32)), "n")
        g.sel_dram, g.d = d["sel"], d

        def first(sp, s):
            sp.dma_start(g.x[:, :, :], d["hidden"].rearrange("(j p) d -> p j d", p=P)).then_inc(s, 16)
            sp.dma_start(g.ident[:, :], d["ident"]).then_inc(s, 16)
            return 2

        modulation(nc, g, 0, d["c0"], d["wmod0"], first)
        mamba(nc, g, d["w_in"], d["conv_w"], d["conv_b"], d["xproj"], d["dtw"], d["dtb"], d["a_log"], d["dskip"], d["w_out"])
        moe(nc, g, 0, 688, d["router0"], d["g0"], d["u0"], d["d0"])
        modulation(nc, g, 1, d["c1"], d["wmod1"])
        attn1(nc, g, d["q1"], d["k1"], d["v1"], d["fcw"], d["fcb"])
        hsctx = ExitStack()
        with hsctx:
            hs = hsctx.enter_context(nc.sbuf_tensor("hs", [P, NT, D], F32))
            attn2(nc, g, hs, d["n1"], d["wq"], d["wk"], d["wv"], d["wo"])
            moe(nc, g, 1, 512, d["router1"], d["g1"], d["u1"], d["d1"], hs, d["n2"])
        with nc.Block() as block:
            @block.sync
            def _(sp):
                sp.dma_start(out.rearrange("(j p) d -> p j d", p=P), g.x[:, :, :]).then_inc(g.s_io, 16)
                sp.wait_ge(g.s_io, 16 * 3)


def kernel(**inputs):
    import concourse.bacc as _bacc
    from concourse.bass_utils import run_bass_kernel_spmd as _run

    a = {k: np.asarray(v) for k, v in inputs.items()}
    T = np.ascontiguousarray
    chunked = lambda v: T(v.reshape(CD, P).T)
    xp = a["L0_attn_x_proj_w"]
    host = {
        "hidden": T(a["L0_attn_hidden_states"].reshape(B * L, D)),
        "ident": np.eye(P, dtype=np.float32),
        "sel": np.tile(np.eye(32, dtype=np.float32), (3, 1)),
        "c0": T(a["L0_c"]), "wmod0": T(a["L0_wmod"]), "c1": T(a["L1_c"]), "wmod1": T(a["L1_wmod"]),
        "w_in": T(a["L0_attn_in_proj_w"].T), "conv_w": T(a["L0_attn_conv_w"]), "conv_b": chunked(a["L0_attn_conv_b"]),
        "xproj": T(np.concatenate([xp[DTR:], xp[:DTR]], 0).T), "dtw": T(a["L0_attn_dt_proj_w"].T),
        "dtb": chunked(a["L0_attn_dt_proj_b"]), "a_log": T(a["L0_attn_A_log"]), "dskip": chunked(a["L0_attn_D"]),
        "w_out": T(a["L0_attn_out_proj_w"].T),
    }
    k = np.arange
    row16 = (k(NT) * P).astype(np.float32)
    row16[0] = 3e38
    wide = lambda v: T(np.broadcast_to(v.reshape(1, -1).astype(np.float32), (P, v.size)))
    freq = np.float32(1.0) / np.power(np.float32(1e6), k(0, HD, 2, dtype=np.float32) / np.float32(HD))
    ang = (k(L, dtype=np.float32)[:, None] * freq[None, :]).T
    host.update({
        "cos": np.concatenate([np.cos(ang), np.cos(ang)], 0).astype(np.float32),
        "sin": np.concatenate([np.sin(ang), -np.sin(ang)], 0).astype(np.float32),
        "mask": np.where(k(P)[None, :] > k(P)[:, None], np.float32(-3e38), np.float32(0)).astype(np.float32),
        "tri": (k(P)[:, None] < k(P)[None, :]).astype(np.float32), "ones": np.ones((P, P), np.float32),
        "e8": wide(k(EXP)), "row16": wide(row16), "row40": wide(k(SLOT_TILES)),
        "low8": wide((k(EXP)[None, :] < k(EXP)[:, None]).astype(np.float32)),
        "router0": T(a["L0_ffn_router_w"].T), "g0": T(a["L0_ffn_gate_w"].transpose(0, 2, 1)),
        "u0": T(a["L0_ffn_up_w"].transpose(0, 2, 1)), "d0": T(a["L0_ffn_down_w"].transpose(0, 2, 1)),
        "router1": T(a["L1_ffn_gate_w"]), "g1": T(a["L1_ffn_w1"]), "u1": T(a["L1_ffn_w3"]), "d1": T(a["L1_ffn_w2"]),
        "n1": T(a["L1_ffn_norm1_w"]), "n2": T(a["L1_ffn_norm2_w"]),
        "wq": T(a["L1_ffn_wq"]), "wk": T(a["L1_ffn_wk"]), "wv": T(a["L1_ffn_wv"]), "wo": T(a["L1_ffn_wo"]),
        "q1": T(a["L1_attn_Wq"].transpose(2, 0, 1).reshape(D, AH * D)),
        "k1": T(a["L1_attn_Wk"].transpose(2, 0, 1).reshape(D, AH * D)),
        "v1": T(a["L1_attn_Wv"].transpose(2, 0, 1).reshape(D, AH * D)),
        "fcw": T(a["L1_attn_fc_w"].T), "fcb": T(a["L1_attn_fc_b"].reshape(1, D)),
    })
    nc = _bacc.Bacc("TRN2", target_bir_lowering=False, num_devices=1)
    d = {k: nc.dram_tensor(f"in_{k}", v.shape, mybir.dt.from_np(v.dtype), kind="ExternalInput").ap() for k, v in host.items()}
    out = nc.dram_tensor("out_x", (B * L, D), F32, kind="ExternalOutput").ap()
    program(nc, d, out)
    r = _run(nc, [{f"in_{k}": v for k, v in host.items()}], core_ids=[0])
    return r.results[0]["out_x"].reshape(B, L, D)
```
